# Optimizing a Trainium2 kernel written in Bass

```python
import numpy as np
import jax
import jax.numpy as jnp

def _softmax(x, axis=-1):
    return jax.nn.softmax(x, axis=axis)

def _gelu(x):
    return jax.nn.gelu(x, approximate=True)

def _silu(x):
    return jax.nn.silu(x)

def _sigmoid(x):
    return jax.nn.sigmoid(x)

def _layernorm(x, axis=-1, eps=1e-05):
    m = jnp.mean(x, axis=axis, keepdims=True)
    v = jnp.var(x, axis=axis, keepdims=True)
    return (x - m) / jnp.sqrt(v + eps)

def _scatter_add(tgt, idx, src, axis=0):
    return tgt.at[idx].add(src)

def _segment_sum(src, seg, n):
    return jax.ops.segment_sum(src, seg, n)
kernel_name = 'mk_gps_d2_gnn_r64_6ef481'

def setup_inputs(seed: int=0):
    np.random.seed(seed)
    _w = jnp.asarray

    def _rec_inputs():
        import jax
        import jax.numpy as jnp
        _gk = jax.random.key(seed)
        x = -0.0002928 + 1 * jax.random.normal(jax.random.fold_in(_gk, 1), (128, 512), jnp.float32)
        src = jax.random.randint(jax.random.fold_in(_gk, 2), (2048,), 0, 128, jnp.int32)
        dst = jax.random.randint(jax.random.fold_in(_gk, 3), (2048,), 0, 128, jnp.int32)
        _o = jnp.argsort(dst, stable=True)
        src = src[_o]
        dst = dst[_o]
        edge_weight = jax.random.uniform(jax.random.fold_in(_gk, 12), (2048,), jnp.float32, 0.0, 0.999994)
        return (x, src, dst, edge_weight)
    x, src, dst, edge_weight = _rec_inputs()

    def _L0_gnn_setup():
        import jax, jax.numpy as jnp
        import numpy as np
        N_NODES = 128
        D_MODEL = 512
        N_LAYERS = 2
        N_EDGES = 4096
        LEAKY_SLOPE = 0.01

        def _normalized_adj(edge_index, edge_weights, num_nodes):
            A = jnp.zeros((num_nodes, num_nodes), dtype=edge_weights.dtype)
            A = A.at[edge_index[0], edge_index[1]].add(edge_weights)
            deg = jnp.sum(A, axis=1)
            dinv = jnp.where(deg > 0, deg ** (-0.5), 0.0)
            return dinv[:, None] * A * dinv[None, :]
        key = jax.random.key(seed)
        ks = jax.random.split(key, 6)
        x = jax.random.normal(ks[0], (N_NODES, D_MODEL), dtype=jnp.float32)
        edge_weights = jax.random.uniform(ks[1], (N_EDGES,), dtype=jnp.float32)
        edge_index = jax.random.randint(ks[2], (2, N_EDGES), 0, N_NODES, dtype=jnp.int64)
        scale = 0.02
        W_gcn = jax.random.normal(ks[3], (N_LAYERS, D_MODEL, D_MODEL), dtype=jnp.float32) * scale
        b_gcn = jnp.zeros((N_LAYERS, D_MODEL), dtype=jnp.float32)
        W_mlp = jax.random.normal(ks[4], (N_LAYERS, D_MODEL, D_MODEL), dtype=jnp.float32) * scale
        b_mlp = jnp.zeros((N_LAYERS, D_MODEL), dtype=jnp.float32)
        return {'x': x, 'edge_weights': edge_weights, 'W_gcn': W_gcn, 'b_gcn': b_gcn, 'W_mlp': W_mlp, 'b_mlp': b_mlp, 'edge_index': edge_index}
    _L0_gnn_all = _L0_gnn_setup()
    _L0_gnn_in = {k: v for k, v in _L0_gnn_all.items() if k in ('W_gcn', 'b_gcn', 'W_mlp', 'b_mlp')}
    del _L0_gnn_all

    def _L0_mix_setup():
        import jax, jax.numpy as jnp
        import numpy as np
        NUM_HEADS = 8
        EPS = 1e-06
        key = jax.random.key(seed)
        k1, k2, k3 = jax.random.split(key, 3)
        B, N, C = (8, 64, 512)
        x = jax.random.normal(k1, (B, N, C), dtype=jnp.float32)
        Wq = jax.random.normal(k2, (C, C), dtype=jnp.float32) * (1.0 / np.sqrt(C))
        Wkv = jax.random.normal(k3, (2 * C, C), dtype=jnp.float32) * (1.0 / np.sqrt(C))
        return {'x': x, 'Wq': Wq, 'Wkv': Wkv}
    _L0_mix_all = _L0_mix_setup()
    _L0_mix_in = {k: v for k, v in _L0_mix_all.items() if k in ('Wq', 'Wkv')}
    del _L0_mix_all

    def _L0_ffn_setup():
        import jax, jax.numpy as jnp
        import numpy as np
        B, L, H, E, F, C = (8, 128, 512, 8, 1024, 2)
        key = jax.random.key(seed)
        ks = jax.random.split(key, 4)
        x = jax.random.normal(ks[0], (B, L, H), jnp.float32)
        Wg = jax.random.normal(ks[1], (H, E), jnp.float32) * H ** (-0.5)
        W1 = jax.random.normal(ks[2], (E, H, F), jnp.float32) * H ** (-0.5)
        b1 = jnp.zeros((E, F), jnp.float32)
        W2 = jax.random.normal(ks[3], (E, F, H), jnp.float32) * F ** (-0.5)
        b2 = jnp.zeros((E, H), jnp.float32)
        return {'x': x, 'Wg': Wg, 'W1': W1, 'b1': b1, 'W2': W2, 'b2': b2}
    _L0_ffn_all = _L0_ffn_setup()
    _L0_ffn_in = {k: v for k, v in _L0_ffn_all.items() if k in ('Wg', 'W1', 'b1', 'W2', 'b2')}
    del _L0_ffn_all

    def _L1_gnn_setup():
        import jax, jax.numpy as jnp
        import numpy as np
        N = 128
        D = 512
        E = 4096
        STEPS = 3
        key = jax.random.key(seed)
        k1, k2, k3 = jax.random.split(key, 3)
        x = jax.random.normal(k1, (N, D), dtype=jnp.float32)
        edge_index = jax.random.randint(k2, (2, E), 0, N, dtype=jnp.int32)
        W = jax.random.normal(k3, (D, D), dtype=jnp.float32) / np.sqrt(D)
        b = jnp.zeros((D,), dtype=jnp.float32)
        diffusion_weights = jnp.ones((STEPS + 1,), dtype=jnp.float32) / (STEPS + 1)
        return {'x': x, 'edge_index': edge_index, 'W': W, 'b': b, 'diffusion_weights': diffusion_weights}
    _L1_gnn_all = _L1_gnn_setup()
    _L1_gnn_in = {k: v for k, v in _L1_gnn_all.items() if k in ('W', 'b', 'diffusion_weights')}
    del _L1_gnn_all

    def _L1_mix_setup():
        import jax, jax.numpy as jnp
        import numpy as np
        DIM = 512
        NUM_HEADS = 8
        HEAD_DIM = DIM // NUM_HEADS
        EPS = 1e-06

        def _feature_map(x):
            return jax.nn.elu(x) + 1.0
        key = jax.random.key(seed)
        k_x, k_qkv, k_out, k_b = jax.random.split(key, 4)
        B, N = (8, 64)
        x = jax.random.normal(k_x, (B, N, DIM), dtype=jnp.float32)
        s_qkv = 1.0 / np.sqrt(DIM)
        W_qkv = jax.random.uniform(k_qkv, (DIM, 3 * DIM), minval=-s_qkv, maxval=s_qkv, dtype=jnp.float32)
        W_out = jax.random.uniform(k_out, (DIM, DIM), minval=-s_qkv, maxval=s_qkv, dtype=jnp.float32)
        b_out = jax.random.uniform(k_b, (DIM,), minval=-s_qkv, maxval=s_qkv, dtype=jnp.float32)
        return {'x': x, 'W_qkv': W_qkv, 'W_out': W_out, 'b_out': b_out}
    _L1_mix_all = _L1_mix_setup()
    _L1_mix_in = {k: v for k, v in _L1_mix_all.items() if k in ('W_qkv', 'W_out', 'b_out')}
    del _L1_mix_all

    def _L1_ffn_setup():
        import jax, jax.numpy as jnp
        import numpy as np
        E = 16
        K = 4
        NEG = jnp.float32(-1e+20)

        def _swiglu(x, w1, w2, w3):
            a = x @ w1
            return a * jax.nn.sigmoid(a) * (x @ w2) @ w3
        key = jax.random.key(seed)
        ks = jax.random.split(key, 9)
        B, S, D, H = (32, 512, 512, 1365)
        s = 0.02
        return {'x': jax.random.normal(ks[0], (B, S, D), jnp.float32), 'gate_w': jax.random.normal(ks[1], (D, E), jnp.float32) * s, 'routing_bias': jnp.zeros((E,), jnp.float32), 'w1': jax.random.normal(ks[2], (E, D, H), jnp.float32) * s, 'w2': jax.random.normal(ks[3], (E, D, H), jnp.float32) * s, 'w3': jax.random.normal(ks[4], (E, H, D), jnp.float32) * s, 'sw1': jax.random.normal(ks[5], (D, H), jnp.float32) * s, 'sw2': jax.random.normal(ks[6], (D, H), jnp.float32) * s, 'sw3': jax.random.normal(ks[7], (H, D), jnp.float32) * s}
    _L1_ffn_all = _L1_ffn_setup()
    _L1_ffn_in = {k: v for k, v in _L1_ffn_all.items() if k in ('gate_w', 'routing_bias', 'w1', 'w2', 'w3', 'sw1', 'sw2', 'sw3')}
    del _L1_ffn_all
    return {'x': x, 'src': src, 'dst': dst, 'edge_weight': edge_weight, 'L0_gnn_W_gcn': _L0_gnn_in['W_gcn'], 'L0_gnn_b_gcn': _L0_gnn_in['b_gcn'], 'L0_gnn_W_mlp': _L0_gnn_in['W_mlp'], 'L0_gnn_b_mlp': _L0_gnn_in['b_mlp'], 'L0_mix_Wq': _L0_mix_in['Wq'], 'L0_mix_Wkv': _L0_mix_in['Wkv'], 'L0_ffn_Wg': _L0_ffn_in['Wg'], 'L0_ffn_W1': _L0_ffn_in['W1'], 'L0_ffn_b1': _L0_ffn_in['b1'], 'L0_ffn_W2': _L0_ffn_in['W2'], 'L0_ffn_b2': _L0_ffn_in['b2'], 'L1_gnn_W': _L1_gnn_in['W'], 'L1_gnn_b': _L1_gnn_in['b'], 'L1_gnn_diffusion_weights': _L1_gnn_in['diffusion_weights'], 'L1_mix_W_qkv': _L1_mix_in['W_qkv'], 'L1_mix_W_out': _L1_mix_in['W_out'], 'L1_mix_b_out': _L1_mix_in['b_out'], 'L1_ffn_gate_w': _L1_ffn_in['gate_w'], 'L1_ffn_routing_bias': _L1_ffn_in['routing_bias'], 'L1_ffn_w1': _L1_ffn_in['w1'], 'L1_ffn_w2': _L1_ffn_in['w2'], 'L1_ffn_w3': _L1_ffn_in['w3'], 'L1_ffn_sw1': _L1_ffn_in['sw1'], 'L1_ffn_sw2': _L1_ffn_in['sw2'], 'L1_ffn_sw3': _L1_ffn_in['sw3']}

def reference(x, src, dst, edge_weight, L0_gnn_W_gcn, L0_gnn_b_gcn, L0_gnn_W_mlp, L0_gnn_b_mlp, L0_mix_Wq, L0_mix_Wkv, L0_ffn_Wg, L0_ffn_W1, L0_ffn_b1, L0_ffn_W2, L0_ffn_b2, L1_gnn_W, L1_gnn_b, L1_gnn_diffusion_weights, L1_mix_W_qkv, L1_mix_W_out, L1_mix_b_out, L1_ffn_gate_w, L1_ffn_routing_bias, L1_ffn_w1, L1_ffn_w2, L1_ffn_w3, L1_ffn_sw1, L1_ffn_sw2, L1_ffn_sw3):
    import jax
    import jax.numpy as jnp

    def _L0_gnn_ref(x, edge_weights, W_gcn, b_gcn, W_mlp, b_mlp, edge_index):
        import jax, jax.numpy as jnp
        import numpy as np
        N_NODES = 128
        D_MODEL = 512
        N_LAYERS = 2
        N_EDGES = 4096
        LEAKY_SLOPE = 0.01

        def _normalized_adj(edge_index, edge_weights, num_nodes):
            A = jnp.zeros((num_nodes, num_nodes), dtype=edge_weights.dtype)
            A = A.at[edge_index[0], edge_index[1]].add(edge_weights)
            deg = jnp.sum(A, axis=1)
            dinv = jnp.where(deg > 0, deg ** (-0.5), 0.0)
            return dinv[:, None] * A * dinv[None, :]
        N = x.shape[0]
        A_norm = _normalized_adj(edge_index, edge_weights, N)
        h = x
        for l in range(W_gcn.shape[0]):
            h = A_norm @ h
            h = h @ W_gcn[l] + b_gcn[l]
            h = jax.nn.leaky_relu(h @ W_mlp[l] + b_mlp[l], negative_slope=LEAKY_SLOPE)
        return h

    def _L0_mix_ref(x, Wq, Wkv):
        import jax, jax.numpy as jnp
        import numpy as np
        NUM_HEADS = 8
        EPS = 1e-06
        B, N, C = x.shape
        h = NUM_HEADS
        d = C // h
        q = (x @ Wq.T).reshape(B, N, h, d)
        kv = (x @ Wkv.T).reshape(B, N, 2, h, d)
        k = kv[:, :, 0]
        v = kv[:, :, 1]
        Q = jax.nn.elu(q) + 1.0
        K = jax.nn.elu(k) + 1.0
        v_length = v.shape[1]
        v = v / v_length
        KV = jnp.einsum('nshd,nshv->nhdv', K, v)
        Z = 1.0 / (jnp.einsum('nlhd,nhd->nlh', Q, K.sum(axis=1)) + EPS)
        out = jnp.einsum('nlhd,nhdv,nlh->nlhv', Q, KV, Z) * v_length
        return out.reshape(B, N, C)

    def _L0_ffn_ref(x, Wg, W1, b1, W2, b2):
        import jax, jax.numpy as jnp
        import numpy as np
        B, L, H, E, F, C = (8, 128, 512, 8, 1024, 2)
        b, l, h = x.shape
        e = Wg.shape[1]
        k = min(max(int(l * C / e), 1), l)
        S = jax.nn.softmax(x @ Wg, axis=-1)
        St = jnp.swapaxes(S, 1, 2)
        G, I = jax.lax.top_k(St, k)
        ex = jnp.take_along_axis(x[:, None], I[..., None], axis=2)
        hmid = jax.nn.gelu(jnp.einsum('bekh,ehf->bekf', ex, W1) + b1[None, :, None, :], approximate=False)
        out = jnp.einsum('bekf,efh->bekh', hmid, W2) + b2[None, :, None, :]
        vals = G[..., None] * out
        new_x = jnp.zeros_like(x).at[jnp.arange(b)[:, None, None], I].add(vals)
        return new_x

    def _L1_gnn_ref(x, edge_index, W, b, diffusion_weights):
        import jax, jax.numpy as jnp
        import numpy as np
        N = 128
        D = 512
        E = 4096
        STEPS = 3
        h = x @ W + b
        row, col = (edge_index[0], edge_index[1])
        adj = jnp.zeros((N, N), dtype=h.dtype)
        adj = adj.at[row, col].set(1.0)
        adj = adj.at[col, row].set(1.0)
        adj = adj + jnp.eye(N, dtype=h.dtype)
        row_sum = adj.sum(axis=1, keepdims=True)
        adj = adj / jnp.maximum(row_sum, 1.0)
        out = diffusion_weights[0] * h
        cur = h
        for i in range(STEPS):
            cur = adj @ cur
            out = out + diffusion_weights[i + 1] * cur
        return jax.nn.relu(out)

    def _L1_mix_ref(x, W_qkv, W_out, b_out):
        import jax, jax.numpy as jnp
        import numpy as np
        DIM = 512
        NUM_HEADS = 8
        HEAD_DIM = DIM // NUM_HEADS
        EPS = 1e-06

        def _feature_map(x):
            return jax.nn.elu(x) + 1.0
        B, N, C = x.shape
        H, D = (NUM_HEADS, HEAD_DIM)
        qkv = x @ W_qkv
        qkv = qkv.reshape(B, N, 3, H, D).transpose(2, 0, 3, 1, 4)
        q, k, v = (qkv[0], qkv[1], qkv[2])
        q_phi = _feature_map(q)
        k_phi = _feature_map(k)
        KV = jnp.einsum('bhnd,bhne->bhde', k_phi, v)
        K_sum = k_phi.sum(axis=2)
        denom = jnp.einsum('bhnd,bhd->bhn', q_phi, K_sum)[..., None] + EPS
        out = jnp.einsum('bhnd,bhde->bhne', q_phi, KV) / denom
        out = out.transpose(0, 2, 1, 3).reshape(B, N, C)
        return out @ W_out + b_out

    def _L1_ffn_ref(x, gate_w, routing_bias, w1, w2, w3, sw1, sw2, sw3):
        import jax, jax.numpy as jnp
        import numpy as np
        E = 16
        K = 4
        NEG = jnp.float32(-1e+20)

        def _swiglu(x, w1, w2, w3):
            a = x @ w1
            return a * jax.nn.sigmoid(a) * (x @ w2) @ w3
        gate_out = x @ gate_w + routing_bias
        top_v, top_i = jax.lax.top_k(gate_out, K)
        chosen = jax.nn.one_hot(top_i, E, dtype=x.dtype).sum(axis=-2)
        masked = jnp.where(chosen > 0, gate_out, NEG)
        probs = jax.nn.softmax(masked, axis=-1)
        weights = probs * chosen
        out = _swiglu(x, sw1, sw2, sw3)
        for e in range(E):
            out = out + _swiglu(x, w1[e], w2[e], w3[e]) * weights[..., e:e + 1]
        return out
    edge_index = jnp.stack([src, dst])
    xn = _layernorm(x, axis=-1)
    x = x + _L0_gnn_ref(xn, edge_weight, L0_gnn_W_gcn, L0_gnn_b_gcn, L0_gnn_W_mlp, L0_gnn_b_mlp, edge_index) + _L0_mix_ref(xn[None], L0_mix_Wq, L0_mix_Wkv)[0]
    x = x + _L0_ffn_ref(_layernorm(x, axis=-1)[None], L0_ffn_Wg, L0_ffn_W1, L0_ffn_b1, L0_ffn_W2, L0_ffn_b2)[0]
    xn = _layernorm(x, axis=-1)
    x = x + _L1_gnn_ref(xn, edge_index, L1_gnn_W, L1_gnn_b, L1_gnn_diffusion_weights) + _L1_mix_ref(xn[None], L1_mix_W_qkv, L1_mix_W_out, L1_mix_b_out)[0]
    x = x + _L1_ffn_ref(_layernorm(x, axis=-1)[None], L1_ffn_gate_w, L1_ffn_routing_bias, L1_ffn_w1, L1_ffn_w2, L1_ffn_w3, L1_ffn_sw1, L1_ffn_sw2, L1_ffn_sw3)[0]
    return x

_drawn_inputs = setup_inputs


def setup_inputs(seed=0):
    import zlib

    import numpy as np

    out = dict(_drawn_inputs(seed))
    spreads = {'L0_gnn_b_gcn': (0.0, 0.1),
     'L0_gnn_b_mlp': (0.0, 0.1),
     'L0_ffn_b1': (0.0, 0.27),
     'L0_ffn_b2': (0.0, 0.1),
     'L1_gnn_b': (0.0, 0.1),
     'L1_gnn_diffusion_weights': (0.25, 0.2),
     'L1_ffn_routing_bias': (0.0, 0.485)}
    factors = {'edge_weight': 8.0, 'L0_gnn_W_gcn': 3.398, 'L0_mix_Wq': 7.57}
    for name, (base, spread) in spreads.items():
        noise = np.random.default_rng([zlib.crc32(name.encode()), seed]).standard_normal(out[name].shape)
        drawn = base * np.exp(spread * noise) if base else spread * noise
        out[name] = jnp.asarray(drawn.astype(out[name].dtype))
    for name, factor in factors.items():
        out[name] = (out[name] * factor).astype(out[name].dtype)
    return out
```

```python
import numpy as np

import concourse.bass as bass
from concourse import mybir

ALU = mybir.AluOpType
ACT = mybir.ActivationFunctionType
AX_X = mybir.AxisListType.X
F32 = mybir.dt.float32
F32R = mybir.dt.float32r
I32 = mybir.dt.int32

P = 128
D = 512
KT = D // P
EDGES = 2048
ET = EDGES // P
EQ = 4
HEADS = 8
DH = D // HEADS
PAIRS = HEADS // 2
PW = 2 * (DH + 1)
E0 = 8
F0 = 1024
TOP0 = max(P * 2 // E0, 1)
EG = P // TOP0
GROUPS = E0 // EG
CHUNKS0 = F0 // D
E1 = 16
K1 = 4
F1 = 1365
CHUNK = [(0, 512), (512, 512), (1024, F1 - 1024)]
NC = len(CHUNK)
G_ALL = NC * (E1 + 1)
LN_EPS = 1e-5
ATT_EPS = 1e-6
LEAK = 0.01
TINY = 1e-37


def even(n):
    return n + n % 2


def up32(n):
    return -(-n // 32) * 32


def gps_kernel(nc, x, src, dst, edge_weight, gcn_w, gcn_b, mlp_w, mlp_b, wq, wkv, wg0, w1_0, b1_0, w2_0, b2_0,
               gnn_w, gnn_b, diffusion, wqkv, wout, bout, gate_w, gate_b, w1, w2, w3, sw1, sw2, sw3, out):
    base = up32(nc.sbuf_base)
    size_a = 2 * EG * KT * D * 4
    at_a = base
    size_raw = 2 * up32(KT * F1 * 4) + (2 * KT + 3) * D * 4
    at_b = at_a + size_a
    size_b = max(size_a, size_raw)
    at_c = at_b + size_b
    size_c = 4 * KT * D * 4
    at_d = at_c + size_c

    def place(name, shape, dt, at):
        return nc.alloc_sbuf_tensor_at(name, shape, dt, offset=at)

    class Cursor:

        def __init__(self, at):
            self.at = at

        def __call__(self, name, shape, dt=F32):
            t = place(name, shape, dt, self.at)
            self.at += up32(int(np.prod(shape[1:])) * 4)
            return t

    unit_w1 = [place("unit_w1_a", [P, KT, EG, D], F32, at_a), place("unit_w1_b", [P, KT, EG, D], F32, at_b)]
    unit_w2 = [place("unit_w2_a", [P, KT, EG, D], F32, at_a + size_a // 2),
               place("unit_w2_b", [P, KT, EG, D], F32, at_b + size_a // 2)]
    c = Cursor(at_a + size_a // 2)
    hot_src = [c(f"hot_src{i}", [P, EQ, P]) for i in range(2)]
    hot_dst = [c(f"hot_dst{i}", [P, EQ, 2, P]) for i in range(2)]
    c = Cursor(at_a)
    wqkv_sb = c("wqkv_sb", [P, KT, 3 * D])
    gnn_w_sb = c("gnn_w_sb", [P, KT, D])
    wout_sb = c("wout_sb", [P, KT, D])
    gnn_b_row = c("gnn_b_row", [1, D])
    bout_row = c("bout_row", [1, D])
    c = Cursor(at_b)
    wq_raw = c("wq_raw", [P, KT, D])
    wkv_raw = c("wkv_raw", [P, 2 * KT, D])
    gcn_w_sb = [c(f"gcn_w_sb{i}", [P, KT, D]) for i in range(2)]
    mlp_w_sb = [c(f"mlp_w_sb{i}", [P, KT, D]) for i in range(2)]
    c = Cursor(at_b)
    w1_raw = c("w1_raw", [P, KT, F1])
    w2_raw = c("w2_raw", [P, KT, F1])
    w3_raw = c("w3_raw", [P, 2 * KT + 3, D])
    c = Cursor(at_c)
    wT_sb = c("wT_sb", [P, KT, 3 * D])
    gcn_b_row = c("gcn_b_row", [1, 2, D])
    mlp_b_row = c("mlp_b_row", [1, 2, D])
    c = Cursor(at_c)
    rank_gt = c("rank_gt", [P, E0, P])
    rank_eq = c("rank_eq", [P, E0, P])
    hot_tok = c("hot_tok", [P, EG, TOP0])
    hot_gate = c("hot_gate", [P, EG, TOP0])
    scatter = c("scatter", [P, P])
    exT = c("exT", [P, KT, P])
    mid = [c(f"mid{i}", [P, D]) for i in range(2)]
    midT = [c(f"midT{i}", [P, KT, P]) for i in range(2)]
    unit_out = c("unit_out", [P, D])
    b1_rows = c("b1_rows", [EG, GROUPS, F0])
    b2_sb = c("b2_sb", [E0, D])
    c = Cursor(at_c)
    s1 = [[c("s1_hi0", [P, KT, D], F32R), c("s1_lo0", [P, KT, D], F32R)]]
    s2 = [[c("s2_hi0", [P, KT, D], F32R), c("s2_lo0", [P, KT, D], F32R)]]
    c = Cursor(at_a)
    s1.append([c("s1_hi1", [P, KT, D], F32R), c("s1_lo1", [P, KT, D], F32R)])
    s2.append([c("s2_hi1", [P, KT, D], F32R), c("s2_lo1", [P, KT, D], F32R)])
    s3 = [[c(f"s3_hi{i}", [P, KT, D], F32R), c(f"s3_lo{i}", [P, KT, D], F32R)] for i in range(2)]
    d = Cursor(at_d)
    x0 = d("x0", [P, D])
    x1 = d("x1", [P, D])
    x2 = d("x2", [P, D])
    x3 = x0
    xn = d("xn", [P, D])
    xnT = d("xnT", [P, KT, P])
    xT_hi = d("xT_hi", [P, KT, P], F32R)
    xT_lo = d("xT_lo", [P, KT, P], F32R)
    ident = d("ident", [P, P])
    iota = d("iota", [P, P])
    ones = d("ones", [P, P])
    below = d("below", [P, P])
    below16 = d("below16", [P, E1, E1])
    group_rows = d("group_rows", [EG, P])
    neg_half = d("neg_half", [P, 1])
    adjT = d("adjT", [P, P])
    adj1 = d("adj1", [P, P])
    polyT = d("polyT", [P, P])
    poly_rows = d("poly_rows", [1, P])
    gate0_w = d("gate0_w", [P, KT, E0])
    gate1_w = d("gate1_w", [P, KT, E1])
    gate1_b = d("gate1_b", [1, E1])
    diff_w = d("diff_w", [P, 4])
    src_i = d("src_i", [P, ET], I32)
    dst_i = d("dst_i", [P, ET], I32)
    src_f = d("src_f", [P, ET])
    dst_f = d("dst_f", [P, ET])
    ew = d("ew", [P, ET])
    stats = d("stats", [P, 6])
    mean_var = d("mean_var", [P, 2])
    var_eps = d("var_eps", [P, 1])
    rstd = d("rstd", [P, 1])
    deg = d("deg", [P, 4])
    probs0 = d("probs0", [P, E0])
    masked0 = d("masked0", [P, E0])
    masked0T = d("masked0T", [E0, P])
    rank0 = d("rank0", [P, E0])
    small = d("small", [P, 8])
    logits1 = d("logits1", [P, E1])
    rank1 = d("rank1", [P, E1])
    weights1 = d("weights1", [P, 1 + E1])
    recip = d("recip", [P, HEADS])
    rank_t = [d(f"rank_t{i}", [P, E1, E1]) for i in range(2)]
    at_e = d.at
    h = [d(f"h{i}", [P, D]) for i in range(2)]
    act_a = [d(f"act_a{i}", [P, D]) for i in range(2)]
    hT = [[d(f"hT_hi{i}", [P, KT, P], F32R), d(f"hT_lo{i}", [P, KT, P], F32R)] for i in range(2)]
    e = Cursor(at_e)
    q_phi = e("q_phi", [P, PAIRS, P])
    k_phi = e("k_phi", [P, D])
    v_aug = e("v_aug", [P, HEADS, DH + 1])
    kv_diag = e("kv_diag", [P, PAIRS, PW])
    neg_q = e("neg_q", [P, D])
    neg_k = e("neg_k", [P, D])
    mix = e("mix", [P, D])
    ahT = e("ahT", [P, KT, P])
    gcnT = e("gcnT", [P, KT, P])
    mixT = gcnT
    leak = neg_q
    gnn = e("gnn", [P, D])
    poly_a = e("poly_a", [P, 3, P])
    cnt = e("cnt", [P, 2, P])
    assert max(d.at, e.at) <= nc.sbuf_usable_end, (d.at, e.at)

    ps = nc.alloc_psum_tensor("ps", [P, 8, 512], F32)

    def bank(i):
        return ps[:, i, :]

    def tiles(i):
        return ps[:, i, :].rearrange("p (t n) -> p t n", t=KT)

    def sem(name):
        return nc.alloc_semaphore(name)

    ld_x, ld_edges, ld_small, ld_rows = sem("ld_x"), sem("ld_edges"), sem("ld_small"), sem("ld_rows")
    ld_wq, ld_wkv = sem("ld_wq"), sem("ld_wkv")
    ld_gcn = [sem(f"ld_gcn{i}") for i in range(2)]
    ld_mlp = [sem(f"ld_mlp{i}") for i in range(2)]
    ld_b = sem("ld_b")
    ld_u1 = [[sem(f"ld_u1_{r}{t}") for t in range(KT)] for r in range(2)]
    ld_u2 = [[sem(f"ld_u2_{r}{t}") for t in range(KT)] for r in range(2)]
    ld_gnn_w, ld_wout, ld_l1_rows = sem("ld_gnn_w"), sem("ld_wout"), sem("ld_l1_rows")
    ld_qkv = [sem(f"ld_qkv{i}") for i in range(3)]
    ld_w1 = [sem(f"ld_w1_{i}") for i in range(NC)]
    ld_w2 = [sem(f"ld_w2_{i}") for i in range(NC)]
    ld_w3 = [sem(f"ld_w3_{i}") for i in range(NC)]
    consts = sem("consts")
    pool_seq = sem("pool_seq")
    seq = sem("seq")
    var_ready, rstd_ready = sem("var_ready"), sem("rstd_ready")
    deg_ready, dinv_ready = sem("deg_ready"), sem("dinv_ready")
    xn_ready, xnT_ps, xnT_ready = sem("xn_ready"), sem("xnT_ps"), sem("xnT_ready")
    hot_ready, hot_used = sem("hot_ready"), sem("hot_used")
    adj1_ready, adjT_ps, adjT_ready = sem("adj1_ready"), sem("adjT_ps"), sem("adjT_ready")
    wT_ps, wT_act, wT_dve = sem("wT_ps"), sem("wT_act"), sem("wT_dve")
    q_ps, k_ps, v_ps = sem("q_ps"), sem("k_ps"), sem("v_ps")
    negq_ready, negk_ready, expq_ready, expk_ready = (sem(n) for n in ("negq_ready", "negk_ready", "expq_ready", "expk_ready"))
    qphi_ready, kphi_ready, v_ready = sem("qphi_ready"), sem("kphi_ready"), sem("v_ready")
    kv_ps, kv_ready, att_ps, mix_ready = sem("kv_ps"), sem("kv_ready"), sem("att_ps"), sem("mix_ready")
    ah_ps, ah_ready, gcn_ps, gcn_ready = sem("ah_ps"), sem("ah_ready"), sem("gcn_ps"), sem("gcn_ready")
    mlp_ps, leak_ready, gnn_ready = sem("mlp_ps"), sem("leak_ready"), sem("gnn_ready")
    gate0_ps, max0_ready, exp0_ready, probs_ready = sem("gate0_ps"), sem("max0_ready"), sem("exp0_ready"), sem("probs_ready")
    probs_bc, masked_ready, maskedT_ps, maskedT_ready = sem("probs_bc"), sem("masked_ready"), sem("maskedT_ps"), sem("maskedT_ready")
    poly_ps, poly_ready, polyrow_ready = sem("poly_ps"), sem("poly_ready"), sem("polyrow_ready")
    tok_ready, gather_ps, exT_ready, scatter_ready = sem("tok_ready"), sem("gather_ps"), sem("exT_ready"), sem("scatter_ready")
    mid_ps, mid_ready, midT_ps, midT_ready = sem("mid_ps"), sem("mid_ready"), sem("midT_ps"), sem("midT_ready")
    unit_free = [sem(f"unit_free_{r}") for r in "ab"]
    unit_ready, ffn0_ps = sem("unit_ready"), sem("ffn0_ps")
    gnn1_ps, mixT_ps, mixT_ready, wout_ps = sem("gnn1_ps"), sem("mixT_ps"), sem("mixT_ready"), sem("wout_ps")
    x_hi_ready, x_lo_ready = sem("x_hi_ready"), sem("x_lo_ready")
    gate1_ps, negmax1_ready, exp1_ready, weights_ready = sem("gate1_ps"), sem("negmax1_ready"), sem("exp1_ready"), sem("weights_ready")
    s1_hi, s1_lo, s2_hi, s2_lo, s3_hi, s3_lo = (sem(n) for n in ("s1_hi", "s1_lo", "s2_hi", "s2_lo", "s3_hi", "s3_lo"))
    a_done, b_done, act_ready, h_ready = sem("a_done"), sem("b_done"), sem("act_ready"), sem("h_ready")
    hT_ps, hT_hi_ready, hT_lo_ready, down_done = sem("hT_ps"), sem("hT_hi_ready"), sem("hT_lo_ready"), sem("down_done")
    out_ready, out_stored = sem("out_ready"), sem("out_stored")
    N_CONSTS = 7

    def by_tile(w):
        return w.rearrange("(t p) n -> p t n", p=P)

    def row(v):
        return v.rearrange("(a n) -> a n", a=1)

    w1_0_v = w1_0.rearrange("e (t p) f -> t p e f", p=P)
    w2_0_v = w2_0.rearrange("e (t p) h -> t p e h", p=P)

    block = nc.Block()
    with block as blk:
        @blk.sync
        def _(sp):
            sp.dma_start(x0[:], x).then_inc(ld_x, 16)
            sp.dma_start(wq_raw[:], by_tile(wq)).then_inc(ld_wq, 16)
            for half in range(2):
                sp.dma_start(wkv_raw[:, KT * half:KT * half + KT], by_tile(wkv[D * half:D * half + D])).then_inc(ld_wkv, 16)
            for i in range(2):
                sp.dma_start(gcn_w_sb[i][:], by_tile(gcn_w[i])).then_inc(ld_gcn[i], 16)
                sp.dma_start(mlp_w_sb[i][:], by_tile(mlp_w[i])).then_inc(ld_mlp[i], 16)

            def load_unit(g, r):
                for t in range(KT):
                    sp.dma_start(unit_w1[r][:, t], w1_0_v[t, :, bass.ds(EG * g, EG), D * r:D * r + D]).then_inc(ld_u1[r][t], 16)
                for t in range(KT):
                    sp.dma_start(unit_w2[r][:, t], w2_0_v[KT * r + t, :, bass.ds(EG * g, EG), :]).then_inc(ld_u2[r][t], 16)

            sp.wait_ge(hot_used, ET // EQ)
            load_unit(0, 0)
            sp.wait_ge(mlp_ps, 2)
            load_unit(0, 1)
            with sp.Fori(1, GROUPS) as g:
                for r in range(2):
                    sp.wait_ge(unit_free[r], g)
                    load_unit(g, r)

            sp.wait_ge(unit_free[0], GROUPS)
            sp.dma_start(gnn_w_sb[:], by_tile(gnn_w)).then_inc(ld_gnn_w, 16)
            for i in range(3):
                sp.dma_start(wqkv_sb[:, :, D * i:D * i + D], by_tile(wqkv[:, D * i:D * i + D])).then_inc(ld_qkv[i], 16)
            sp.dma_start(wout_sb[:], by_tile(wout)).then_inc(ld_wout, 16)
            sp.dma_start(gnn_b_row[:], row(gnn_b)).then_inc(ld_l1_rows, 16)
            sp.dma_start(bout_row[:], row(bout)).then_inc(ld_l1_rows, 16)

            def load_up(dst, w, j, s):
                c0, n = CHUNK[j]
                sp.dma_start(dst[:, :, c0:c0 + n], by_tile(w)[:, :, c0:c0 + n]).then_inc(s[j], 16)

            def load_down(w, j):
                c0, n = CHUNK[j]
                full, rest = n // P, n % P
                sp.dma_start(w3_raw[:, c0 // P:c0 // P + full], by_tile(w[c0:c0 + full * P, :])).then_inc(ld_w3[j], 16)
                if rest:
                    lo, most = c0 + full * P, rest // 16 * 16
                    sp.dma_start(w3_raw[0:most, c0 // P + full], w[lo:lo + most, :]).then_inc(ld_w3[j], 16)
                    sp.dma_start(w3_raw[most:rest, c0 // P + full], w[lo + most:lo + rest, :]).then_inc(ld_w3[j], 16)

            sp.wait_ge(unit_free[1], GROUPS)
            for j in range(NC):
                load_up(w1_raw, sw1, j, ld_w1)
                load_up(w2_raw, sw2, j, ld_w2)
                load_down(sw3, j)

            def one(w, i):
                return w[bass.ds(i, 1)].rearrange("a r n -> (a r) n")

            with sp.Fori(0, E1) as i:
                for j in range(NC):
                    sp.wait_ge(s1_lo, NC * i + j + 1)
                    load_up(w1_raw, one(w1, i), j, ld_w1)
                    sp.wait_ge(s2_lo, NC * i + j + 1)
                    load_up(w2_raw, one(w2, i), j, ld_w2)
                    sp.wait_ge(s3_lo, NC * i + j + 1)
                    load_down(one(w3, i), j)
            sp.wait_ge(out_ready, 1)
            sp.dma_start(out, xn[:]).then_inc(out_stored, 16)
            sp.wait_ge(out_stored, 16)

        @blk.gpsimd
        def _(pool):
            pg = nc.gpsimd
            n = [0]

            def then(ins):
                n[0] += 1
                ins.then_inc(pool_seq, 1)
                pool.wait_ge(pool_seq, n[0])

            pg.iota(iota[:], [[1, P]], base=0, channel_multiplier=0, allow_small_or_imprecise_dtypes=True).then_inc(consts, 1)
            pg.memset(neg_half[:], -0.5).then_inc(consts, 1)
            then(pg.memset(ident[:], 0.0))
            pg.affine_select(out=ident[:], in_=ident[:], compare_op=ALU.not_equal, fill=1.0, base=0,
                             pattern=[[-1, P]], channel_multiplier=1).then_inc(consts, 1)
            pg.memset(ones[:], 1.0).then_inc(consts, 1)
            then(pg.memset(below[:], 1.0))
            pg.affine_select(out=below[:], in_=below[:], compare_op=ALU.is_gt, fill=0.0, base=0,
                             pattern=[[-1, P]], channel_multiplier=1).then_inc(consts, 1)
            then(pg.memset(below16[:], 1.0))
            pg.affine_select(out=below16[:], in_=below16[:], compare_op=ALU.is_gt, fill=0.0, base=0,
                             pattern=[[1, E1], [-1, E1]], channel_multiplier=0).then_inc(consts, 1)
            then(pg.memset(group_rows[:], 0.0))
            v = group_rows[:].rearrange("p (j t) -> p j t", j=EG)
            pg.affine_select(out=v, in_=v, compare_op=ALU.not_equal, fill=1.0, base=0,
                             pattern=[[-1, EG], [0, TOP0]], channel_multiplier=1).then_inc(consts, 1)

            def rsqrt_var(l):
                pool.wait_ge(var_ready, l + 1)
                pg.tensor_tensor(rstd[:], var_eps[:], neg_half[:], ALU.pow).then_inc(rstd_ready, 1)

            pool.wait_ge(consts, 2)
            rsqrt_var(0)
            pool.wait_ge(deg_ready, 1)
            pg.tensor_tensor(deg[:, 1:2], deg[:, 0:1], neg_half[:], ALU.pow).then_inc(dinv_ready, 1)
            for l in range(1, 4):
                rsqrt_var(l)

        @blk.scalar
        def _(act):
            a = nc.scalar
            act.dma_start(src_i[:], src.rearrange("(p t) -> p t", t=ET)).then_inc(ld_edges, 16)
            act.dma_start(dst_i[:], dst.rearrange("(p t) -> p t", t=ET)).then_inc(ld_edges, 16)
            act.dma_start(ew[:], edge_weight.rearrange("(p t) -> p t", t=ET)).then_inc(ld_edges, 16)
            act.dma_start(gcn_b_row[:], gcn_b.rearrange("(a l) n -> a l n", a=1)).then_inc(ld_rows, 16)
            act.dma_start(mlp_b_row[:], mlp_b.rearrange("(a l) n -> a l n", a=1)).then_inc(ld_rows, 16)
            act.dma_start(gate0_w[:], by_tile(wg0)).then_inc(ld_small, 16)
            act.dma_start(gate1_w[:], by_tile(gate_w)).then_inc(ld_small, 16)
            act.dma_start(gate1_b[:], row(gate_b)).then_inc(ld_small, 16)
            act.dma_start(diff_w[:], row(diffusion).to_broadcast([P, 4])).then_inc(ld_small, 16)

            def copy_wT(i):
                act.wait_ge(wT_ps, i + 1)
                a.copy(wT_sb[:, i % KT, D * (i // KT):D * (i // KT) + D], bank(2 + i % 2)).then_inc(wT_act, 1)

            def attention(l):
                act.wait_ge(negq_ready, l + 1)
                a.activation(neg_q[:], neg_q[:], ACT.Exp).then_inc(expq_ready, 1)
                act.wait_ge(negk_ready, l + 1)
                a.activation(neg_k[:], neg_k[:], ACT.Exp).then_inc(expk_ready, 1)
                act.wait_ge(v_ps, l + 1)
                a.copy(v_aug[:, :, 0:DH], bank(4).rearrange("p (h v) -> p h v", h=HEADS)).then_inc(v_ready, 1)

            for i in range(0, 3 * KT, 2):
                copy_wT(i)
            for layer in range(2):
                if layer == 0:
                    attention(0)
                act.wait_ge(ah_ps, layer + 1)
                a.copy(ahT[:], tiles(1)).then_inc(ah_ready, 1)
                act.wait_ge(gcn_ps, layer + 1)
                a.copy(gcnT[:], tiles(7)).then_inc(gcn_ready, 1)
                act.wait_ge(mlp_ps, layer + 1)
                if layer == 1:
                    act.wait_ge(gnn_ready, 1)
                a.mul(leak[:], bank(0), LEAK).then_inc(leak_ready, 1)

            act.wait_ge(max0_ready, 1)
            act.dma_start(b1_rows[:], b1_0.rearrange("(g j) f -> j g f", j=EG)).then_inc(ld_b, 16)
            act.dma_start(b2_sb[:], b2_0).then_inc(ld_b, 16)
            a.activation(probs0[:], bank(1)[:, 0:E0], ACT.Exp, bias=small[:, 0:1],
                         accum_out=small[:, 1:2]).then_inc(exp0_ready, 1)

            with act.Fori(0, GROUPS) as g:
                act.wait_ge(gather_ps, g + 1)
                a.copy(exT[:], tiles(1)).then_inc(exT_ready, 1)
                for r in range(CHUNKS0):
                    act.wait_ge(mid_ps, CHUNKS0 * g + r + 1)
                    a.activation(mid[r][:], bank(3 + r), ACT.Gelu).then_inc(mid_ready, 1)
                act.wait_ge(unit_free[1], g + 1)
                a.copy(unit_out[:], bank(2)).then_inc(unit_ready, 1)

            act.wait_ge(ah_ps, 3)
            a.copy(ahT[:], tiles(1)).then_inc(ah_ready, 1)
            attention(1)

            act.wait_ge(xnT_ps, 4)
            a.copy(xT_hi[:], tiles(4)).then_inc(x_hi_ready, 1)

            def up_hi(s, raw, landed, stage, used, done):
                c0, n = s.cols
                act.wait_ge(landed[s.j], 16 * (s.expert + 1))
                if s.n > 1:
                    act.wait_ge(used, s.g - 1)
                a.copy(stage[s.par][0][:, :, 0:n], raw[:, :, c0:c0 + n]).then_inc(done, 1)

            def down_hi(s):
                act.wait_ge(ld_w3[s.j], (48 if s.rest else 16) * (s.expert + 1))
                if s.n > 1:
                    act.wait_ge(down_done, s.g - 1)
                last = a.copy(s3[s.par][0][:, 0:s.full], w3_raw[:, s.t0:s.t0 + s.full])
                if s.rest:
                    last = a.copy(s3[s.par][0][0:s.rest, s.full], w3_raw[0:s.rest, s.t0 + s.full])
                last.then_inc(s3_hi, 1)

            def silu(s):
                act.wait_ge(a_done, s.g + 1)
                if s.n > 1:
                    act.wait_ge(h_ready, s.g - 1)
                n = s.cols[1]
                a.activation(act_a[s.par][:, 0:n], bank(s.par)[:, 0:n], ACT.Silu).then_inc(act_ready, 1)

            def hT_hi(s):
                act.wait_ge(hT_ps, s.g + 1)
                last = a.copy(hT[s.par][0][:, 0:s.full], tiles(4 + s.par)[:, 0:s.full])
                if s.rest:
                    last = a.copy(hT[s.par][0][0:s.rest, s.full], tiles(4 + s.par)[0:s.rest, s.full])
                last.then_inc(hT_hi_ready, 1)

            def chunk(n, i=None):
                s = Step(n, i)
                up_hi(s, w1_raw, ld_w1, s1, a_done, s1_hi)
                if n > 1:
                    hT_hi(Step(n - 2, i))
                up_hi(s, w2_raw, ld_w2, s2, b_done, s2_hi)
                if n > 0:
                    silu(Step(n - 1, i))
                    down_hi(Step(n - 1, i))

            act.wait_ge(wout_ps, 1)
            for n in range(NC):
                if n == 2:
                    act.wait_ge(negmax1_ready, 1)
                    a.activation(weights1[:, 1:1 + E1], logits1[:], ACT.Exp, bias=small[:, 0:1]).then_inc(exp1_ready, 1)
                chunk(n)
            with act.Fori(0, E1 // 2) as i:
                for n in range(NC, 3 * NC):
                    chunk(n, i)
            hT_hi(Step(G_ALL - 2))
            silu(Step(G_ALL - 1))
            down_hi(Step(G_ALL - 1))
            hT_hi(Step(G_ALL - 1))

        @blk.vector
        def _(dve):
            v = nc.vector
            n_seq = [0]

            def then(ins):
                n_seq[0] += 1
                ins.then_inc(seq, 1)
                dve.wait_ge(seq, n_seq[0])

            def layernorm(l, x_in):
                then(v.bn_stats(stats[:], x_in[:]))
                then(v.bn_aggr(mean_var[:], stats[:]))
                v.tensor_scalar(var_eps[:], mean_var[:, 1:2], LN_EPS, None, ALU.add).then_inc(var_ready, 1)
                dve.wait_ge(rstd_ready, l + 1)
                v.tensor_scalar(xn[:], x_in[:], mean_var[:, 0:1], rstd[:], ALU.subtract, ALU.mult).then_inc(xn_ready, 1)

            def copy_xnT(l, i):
                dve.wait_ge(xnT_ps, l + 1)
                v.tensor_copy(xnT[:], tiles(i)).then_inc(xnT_ready, 1)

            def copy_wT(i):
                dve.wait_ge(wT_ps, i + 1)
                v.tensor_copy(wT_sb[:, i % KT, D * (i // KT):D * (i // KT) + D], bank(2 + i % 2)).then_inc(wT_dve, 1)

            def phi(l):
                dve.wait_ge(q_ps, l + 1)
                v.tensor_scalar(neg_q[:], bank(2), 0.0, None, ALU.min).then_inc(negq_ready, 1)
                dve.wait_ge(k_ps, l + 1)
                v.tensor_scalar(neg_k[:], bank(3), 0.0, None, ALU.min).then_inc(negk_ready, 1)
                dve.wait_ge(expq_ready, l + 1)
                v.scalar_tensor_tensor(q_phi[:].rearrange("p a n -> p (a n)"), bank(2), 0.0, neg_q[:],
                                       ALU.max, ALU.add).then_inc(qphi_ready, 1)
                dve.wait_ge(expk_ready, l + 1)
                v.scalar_tensor_tensor(k_phi[:], bank(3), 0.0, neg_k[:], ALU.max, ALU.add).then_inc(kphi_ready, 1)

            def keep_diagonal(l):
                dve.wait_ge(kv_ps, l + 1)
                kv = ps[:, 5:7, 0:2 * PW].rearrange("p b (i c) -> p b i c", i=2)
                own = kv_diag[:].rearrange("p (b i) c -> p b i c", i=2)
                for half in range(2):
                    rows, cols = slice(DH * half, DH * half + DH), slice(PW // 2 * half, PW // 2 * half + PW // 2)
                    last = v.tensor_copy(own[rows, :, :, cols], kv[rows, :, :, cols])
                last.then_inc(kv_ready, 1)

            def attended(l):
                dve.wait_ge(att_ps, l + 1)
                o = ps[:, 3:5, 0:2 * PW].rearrange("p b (h c) -> p b h c", h=HEADS // 2)
                r = recip[:].rearrange("p (b h) -> p b h", b=2)
                then(v.tensor_scalar(r, o[:, :, :, DH], ATT_EPS, None, ALU.add))
                then(v.reciprocal(recip[:], recip[:]))
                v.tensor_tensor(mix[:].rearrange("p (b h c) -> p b h c", b=2, c=DH), o[:, :, :, 0:DH],
                                r.unsqueeze(3).to_broadcast([P, 2, HEADS // 2, DH]), ALU.mult).then_inc(mix_ready, 1)

            def leaky(layer):
                dve.wait_ge(leak_ready, layer + 1)
                v.tensor_tensor(gnn[:], bank(0), leak[:], ALU.max).then_inc(gnn_ready, 1)

            v.memset(kv_diag[:], 0.0)
            v.memset(v_aug[:, :, DH:DH + 1], 1.0)
            v.memset(weights1[:, 0:1], 1.0)
            dve.wait_ge(ld_x, 16)
            layernorm(0, x0)

            dve.wait_ge(ld_edges, 48)
            v.tensor_copy(src_f[:], src_i[:])
            then(v.tensor_copy(dst_f[:], dst_i[:]))
            dve.wait_ge(consts, N_CONSTS)
            cols = iota[:].unsqueeze(1).to_broadcast([P, EQ, P])
            for q in range(ET // EQ):
                def of_edge(t):
                    return t[:, EQ * q:EQ * q + EQ].unsqueeze(2).to_broadcast([P, EQ, P])
                if q == 2:
                    copy_wT(1)
                    copy_wT(3)
                if q > 1:
                    dve.wait_ge(hot_used, q - 1)
                v.tensor_tensor(hot_src[q % 2][:], cols, of_edge(src_f), ALU.is_equal)
                then(v.tensor_tensor(hot_dst[q % 2][:, :, 1], cols, of_edge(dst_f), ALU.is_equal))
                v.tensor_tensor(hot_dst[q % 2][:, :, 0], hot_dst[q % 2][:, :, 1], of_edge(ew), ALU.mult).then_inc(hot_ready, 1)
            dve.wait_ge(hot_used, ET // EQ)
            v.tensor_scalar(cnt[:, 0], bank(7)[:, P:2 * P], 1.0, None, ALU.min)
            then(v.tensor_reduce(deg[:, 2:3], bank(7)[:, 0:P], AX_X, ALU.add))
            v.tensor_scalar(deg[:, 0:1], deg[:, 2:3], TINY, None, ALU.max).then_inc(deg_ready, 1)
            then(v.tensor_scalar(deg[:, 3:4], deg[:, 2:3], 0.0, None, ALU.is_gt))
            dve.wait_ge(dinv_ready, 1)
            then(v.tensor_tensor(deg[:, 2:3], deg[:, 1:2], deg[:, 3:4], ALU.mult))
            v.tensor_scalar(adj1[:], bank(7)[:, 0:P], deg[:, 2:3], None, ALU.mult).then_inc(adj1_ready, 1)
            for i in (5, 7):
                copy_wT(i)
            dve.wait_ge(adjT_ps, 1)
            v.tensor_scalar(adjT[:], bank(1)[:, 0:P], deg[:, 2:3], None, ALU.mult)
            v.tensor_tensor(cnt[:, 1], bank(1)[:, P:2 * P], cnt[:, 0], ALU.add).then_inc(adjT_ready, 1)
            for i in (9, 11):
                copy_wT(i)

            copy_xnT(0, 0)
            phi(0)
            keep_diagonal(0)
            leaky(0)
            attended(0)
            dve.wait_ge(mix_ready, 1)
            v.tensor_tensor(x1[:], x0[:], mix[:], ALU.add)
            leaky(1)
            dve.wait_ge(gnn_ready, 2)
            then(v.tensor_tensor(x1[:], x1[:], gnn[:], ALU.add))

            layernorm(1, x1)
            copy_xnT(1, 0)
            dve.wait_ge(gate0_ps, 1)
            then(v.reduce_max(small[:, 2:3], bank(1)[:, 0:E0], AX_X))
            v.tensor_scalar(small[:, 0:1], small[:, 2:3], -1.0, None, ALU.mult).then_inc(max0_ready, 1)
            dve.wait_ge(exp0_ready, 1)
            then(v.reciprocal(small[:, 3:4], small[:, 1:2]))
            v.tensor_scalar(probs0[:], probs0[:], small[:, 3:4], None, ALU.mult).then_inc(probs_ready, 1)
            dve.wait_ge(probs_bc, 1)
            every = ps[:, 5:7, :].rearrange("p b (e m) -> p (b e) m", m=P)
            own = probs0[:].unsqueeze(2).to_broadcast([P, E0, P])
            v.tensor_tensor(rank_gt[:], every, own, ALU.is_gt)
            then(v.tensor_tensor(rank_eq[:], every, own, ALU.is_equal))
            then(v.tensor_tensor(rank_eq[:], rank_eq[:], below[:].unsqueeze(1).to_broadcast([P, E0, P]), ALU.mult))
            then(v.tensor_tensor(rank_gt[:], rank_gt[:], rank_eq[:], ALU.add))
            then(v.tensor_reduce(rank0[:], rank_gt[:], AX_X, ALU.add))
            v.scalar_tensor_tensor(masked0[:], rank0[:], float(TOP0), probs0[:], ALU.is_lt, ALU.mult).then_inc(masked_ready, 1)
            dve.wait_ge(maskedT_ps, 1)
            v.tensor_copy(masked0T[:], bank(1)[0:E0, 0:P]).then_inc(maskedT_ready, 1)

            then(v.tensor_scalar(cnt[:, 1], cnt[:, 1], 1.0, None, ALU.min))
            then(v.tensor_tensor(cnt[:, 1], cnt[:, 1], ident[:], ALU.add))
            then(v.tensor_reduce(small[:, 4:5], cnt[:, 1], AX_X, ALU.add))
            then(v.tensor_scalar(small[:, 4:5], small[:, 4:5], 1.0, None, ALU.max))
            then(v.reciprocal(small[:, 5:6], small[:, 4:5]))
            v.tensor_scalar(poly_a[:, 0], cnt[:, 1], small[:, 5:6], None, ALU.mult).then_inc(poly_ready, 1)
            dve.wait_ge(ld_small, 64)
            then(v.tensor_scalar(polyT[:], ident[:], diff_w[:, 0:1], None, ALU.mult))
            for k in (1, 2):
                dve.wait_ge(poly_ps, k)
                v.tensor_copy(poly_a[:, k], bank(0)[:, P * (k - 1):P * k]).then_inc(poly_ready, 1)
                dve.wait_ge(poly_ready, k + 1)
                then(v.scalar_tensor_tensor(polyT[:], poly_a[:, k], diff_w[:, k:k + 1], polyT[:], ALU.mult, ALU.add))
            dve.wait_ge(poly_ps, 3)
            v.scalar_tensor_tensor(polyT[:], bank(0)[:, 2 * P:3 * P], diff_w[:, 3:4], polyT[:],
                                   ALU.mult, ALU.add).then_inc(poly_ready, 1)
            dve.wait_ge(poly_ps, 4)
            v.tensor_copy(poly_rows[:], bank(0)[0:1, 3 * P:4 * P]).then_inc(polyrow_ready, 1)

            with dve.Fori(0, GROUPS) as g:
                def of_group(t):
                    return t[:, bass.ds(EG * g, EG)].unsqueeze(2).to_broadcast([P, EG, TOP0])
                v.tensor_tensor(hot_tok[:], iota[:, 0:TOP0].unsqueeze(1).to_broadcast([P, EG, TOP0]), of_group(rank0),
                                ALU.is_equal).then_inc(tok_ready, 1)
                dve.wait_ge(tok_ready, 2 * g + 1)
                v.tensor_tensor(hot_gate[:], hot_tok[:], of_group(probs0), ALU.mult).then_inc(tok_ready, 1)
                dve.wait_ge(gather_ps, g + 1)
                v.tensor_copy(scatter[:], bank(0)[:, 0:P]).then_inc(scatter_ready, 1)
                for r in range(CHUNKS0):
                    dve.wait_ge(midT_ps, CHUNKS0 * g + r + 1)
                    v.tensor_copy(midT[r][:], tiles(5 + r)).then_inc(midT_ready, 1)
            dve.wait_ge(ffn0_ps, GROUPS)
            then(v.tensor_tensor(x2[:], bank(7), x1[:], ALU.add))

            layernorm(2, x2)
            copy_xnT(2, 0)
            dve.wait_ge(gnn1_ps, 1)
            v.scalar_tensor_tensor(x1[:], bank(7), 0.0, x2[:], ALU.max, ALU.add)
            phi(1)
            keep_diagonal(1)
            attended(1)
            dve.wait_ge(mixT_ps, 1)
            v.tensor_copy(mixT[:], tiles(0)).then_inc(mixT_ready, 1)
            dve.wait_ge(wout_ps, 1)
            then(v.tensor_tensor(x3[:], bank(1), x1[:], ALU.add))
            layernorm(3, x3)

            dve.wait_ge(x_hi_ready, 1)
            v.tensor_tensor(xT_lo[:], tiles(4), xT_hi[:].bitcast(F32), ALU.subtract).then_inc(x_lo_ready, 1)
            copy_xnT(3, 4)

            def up_lo(s, raw, stage, hi_done, done):
                c0, n = s.cols
                dve.wait_ge(hi_done, s.g + 1)
                hi, lo = stage[s.par]
                v.tensor_tensor(lo[:, :, 0:n], raw[:, :, c0:c0 + n], hi[:, :, 0:n].bitcast(F32), ALU.subtract).then_inc(done, 1)

            def down_lo(s):
                dve.wait_ge(s3_hi, s.g + 1)
                hi, lo = s3[s.par]
                last = v.tensor_tensor(lo[:, 0:s.full], w3_raw[:, s.t0:s.t0 + s.full], hi[:, 0:s.full].bitcast(F32), ALU.subtract)
                if s.rest:
                    last = v.tensor_tensor(lo[0:s.rest, s.full], w3_raw[0:s.rest, s.t0 + s.full],
                                           hi[0:s.rest, s.full].bitcast(F32), ALU.subtract)
                last.then_inc(s3_lo, 1)

            def gated(s):
                dve.wait_ge(act_ready, s.g + 1)
                dve.wait_ge(b_done, s.g + 1)
                if s.n > 1:
                    dve.wait_ge(hT_ps, s.g - 1)
                n = s.cols[1]
                v.scalar_tensor_tensor(h[s.par][:, 0:n], act_a[s.par][:, 0:n], weights1[:, bass.ds(s.expert, 1)],
                                       bank(2 + s.par)[:, 0:n], ALU.mult, ALU.mult).then_inc(h_ready, 1)

            def hT_lo(s):
                dve.wait_ge(hT_hi_ready, s.g + 1)
                hi, lo = hT[s.par]
                last = v.tensor_tensor(lo[:, 0:s.full], tiles(4 + s.par)[:, 0:s.full], hi[:, 0:s.full].bitcast(F32), ALU.subtract)
                if s.rest:
                    last = v.tensor_tensor(lo[0:s.rest, s.full], tiles(4 + s.par)[0:s.rest, s.full],
                                           hi[0:s.rest, s.full].bitcast(F32), ALU.subtract)
                last.then_inc(hT_lo_ready, 1)

            def chunk(n, i=None):
                s = Step(n, i)
                up_lo(s, w1_raw, s1, s1_hi, s1_lo)
                if n > 1:
                    hT_lo(Step(n - 2, i))
                up_lo(s, w2_raw, s2, s2_hi, s2_lo)
                if n > 0:
                    gated(Step(n - 1, i))
                    down_lo(Step(n - 1, i))

            def router():
                dve.wait_ge(gate1_ps, 1)
                then(v.tensor_copy(logits1[:], bank(7)[:, 0:E1]))
                then(v.reduce_max(small[:, 2:3], logits1[:], AX_X))
                v.tensor_scalar(small[:, 0:1], small[:, 2:3], -1.0, None, ALU.mult).then_inc(negmax1_ready, 1)
                other = logits1[:].unsqueeze(1).to_broadcast([P, E1, E1])
                own = logits1[:].unsqueeze(2).to_broadcast([P, E1, E1])
                v.tensor_tensor(rank_t[0][:], other, own, ALU.is_gt)
                then(v.tensor_tensor(rank_t[1][:], other, own, ALU.is_equal))
                then(v.tensor_tensor(rank_t[1][:], rank_t[1][:], below16[:], ALU.mult))
                then(v.tensor_tensor(rank_t[0][:], rank_t[0][:], rank_t[1][:], ALU.add))
                then(v.tensor_reduce(rank1[:], rank_t[0][:], AX_X, ALU.add))
                dve.wait_ge(exp1_ready, 1)
                w = weights1[:, 1:1 + E1]
                then(v.scalar_tensor_tensor(w, rank1[:], float(K1), w, ALU.is_lt, ALU.mult))
                then(v.tensor_reduce(small[:, 6:7], w, AX_X, ALU.add))
                then(v.reciprocal(small[:, 7:8], small[:, 6:7]))
                then(v.tensor_scalar(w, w, small[:, 7:8], None, ALU.mult))

            for n in range(NC):
                if n == 2:
                    router()
                chunk(n)
            with dve.Fori(0, E1 // 2) as i:
                for n in range(NC, 3 * NC):
                    chunk(n, i)
            hT_lo(Step(G_ALL - 2))
            gated(Step(G_ALL - 1))
            down_lo(Step(G_ALL - 1))
            hT_lo(Step(G_ALL - 1))
            dve.wait_ge(down_done, G_ALL)
            v.tensor_tensor(xn[:], bank(6), x3[:], ALU.add).then_inc(out_ready, 1)

        @blk.tensor
        def _(pe):
            t_ = nc.tensor
            mm = t_.matmul

            def transpose_x(l, i):
                pe.wait_ge(xn_ready, l + 1)
                for k in range(KT):
                    last = t_.transpose(tiles(i)[:, k], xn[:, P * k:P * k + P], ident[:])
                last.then_inc(xnT_ps, 1)

            def project(l, w, waits):
                pe.wait_ge(xnT_ready, 2 * l + 1)
                waits(0)
                for m in range(KT):
                    for k in range(KT):
                        last = mm(tiles(2)[:, m], w[:, k, P * m:P * m + P], xnT[:, k], start=(k == 0), stop=(k == KT - 1))
                last.then_inc(q_ps, 1)
                for part, done in ((1, k_ps), (2, v_ps)):
                    waits(part)
                    for k in range(KT):
                        last = mm(bank(2 + part), xnT[:, k], w[:, k, D * part:D * part + D], start=(k == 0), stop=(k == KT - 1))
                    last.then_inc(done, 1)

            def keys_values(l):
                pe.wait_ge(kphi_ready, l + 1)
                pe.wait_ge(v_ready, l + 1)
                for p in range(PAIRS):
                    last = mm(ps[:, 5 + p // 2, PW * (p % 2):PW * (p % 2) + PW], k_phi[:, P * p:P * p + P],
                              v_aug[:, 2 * p:2 * p + 2].rearrange("p h c -> p (h c)"), start=True, stop=True)
                last.then_inc(kv_ps, 1)

            def attend(l):
                pe.wait_ge(kv_ready, l + 1)
                pe.wait_ge(qphi_ready, l + 1)
                for p in range(PAIRS):
                    last = mm(ps[:, 3 + p // 2, PW * (p % 2):PW * (p % 2) + PW], q_phi[:, p], kv_diag[:, p], start=True, stop=True)
                last.then_inc(att_ps, 1)

            def neighbours(rows, adj):
                for k in range(KT):
                    last = mm(tiles(1)[:, k], rows[:, P * k:P * k + P], adj[:], start=True, stop=True)
                last.then_inc(ah_ps, 1)

            def transpose_w(i):
                part, k = i // KT, i % KT
                if i % (KT) == 0:
                    if part == 0:
                        pe.wait_ge(ld_wq, 16)
                    elif part == 1:
                        pe.wait_ge(ld_wkv, 32)
                if i > 1:
                    pe.wait_ge(wT_dve if i % 2 else wT_act, i // 2)
                raw, o0 = (wq_raw, 0) if part == 0 else (wkv_raw, KT * (part - 1))
                for o in range(KT):
                    last = t_.transpose(tiles(2 + i % 2)[:, o], raw[:, o0 + o, P * k:P * k + P], ident[:])
                last.then_inc(wT_ps, 1)

            pe.wait_ge(consts, N_CONSTS)
            for i in range(KT):
                transpose_w(i)
            for q in range(ET // EQ):
                pe.wait_ge(hot_ready, q + 1)
                for t in range(EQ):
                    last = mm(bank(7)[:, 0:2 * P], hot_src[q % 2][:, t], hot_dst[q % 2][:, t].rearrange("p a n -> p (a n)"),
                              start=(q == 0 and t == 0), stop=(q == ET // EQ - 1 and t == EQ - 1))
                last.then_inc(hot_used, 1)
            for i in range(KT, 2 * KT):
                transpose_w(i)
            pe.wait_ge(adj1_ready, 1)
            t_.transpose(bank(1)[:, 0:P], adj1[:], ident[:])
            t_.transpose(bank(1)[:, P:2 * P], cnt[:, 0], ident[:]).then_inc(adjT_ps, 1)
            for i in range(2 * KT, 3 * KT):
                transpose_w(i)

            def waits_T(part):
                if part == 0:
                    pe.wait_ge(wT_act, 3 * KT // 2)
                    pe.wait_ge(wT_dve, 3 * KT // 2)

            def gcn_layer(layer, rows):
                pe.wait_ge(adjT_ready, 1)
                neighbours(rows, adjT)
                pe.wait_ge(ld_gcn[layer], 16)
                pe.wait_ge(ld_rows, 32)
                pe.wait_ge(ah_ready, layer + 1)
                for m in range(KT):
                    for k in range(KT):
                        mm(tiles(7)[:, m], gcn_w_sb[layer][:, k, P * m:P * m + P], ahT[:, k], start=(k == 0), stop=False)
                    last = mm(tiles(7)[:, m], gcn_b_row[:, layer, P * m:P * m + P], ones[0:1, :], start=False, stop=True)
                last.then_inc(gcn_ps, 1)

            def mlp_layer(layer):
                pe.wait_ge(ld_mlp[layer], 16)
                mm(bank(0), ones[0:1, :], mlp_b_row[:, layer], start=True, stop=False)
                pe.wait_ge(gcn_ready, layer + 1)
                for k in range(KT):
                    last = mm(bank(0), gcnT[:, k], mlp_w_sb[layer][:, k], start=False, stop=(k == KT - 1))
                last.then_inc(mlp_ps, 1)

            transpose_x(0, 0)
            project(0, wT_sb, waits_T)
            gcn_layer(0, xn)
            keys_values(0)
            mlp_layer(0)
            attend(0)
            pe.wait_ge(gnn_ready, 1)
            gcn_layer(1, gnn)
            mlp_layer(1)

            transpose_x(1, 0)
            pe.wait_ge(xnT_ready, 2)
            pe.wait_ge(ld_small, 64)
            for k in range(KT):
                last = mm(bank(1)[:, 0:E0], xnT[:, k], gate0_w[:, k], start=(k == 0), stop=(k == KT - 1))
            last.then_inc(gate0_ps, 1)
            pe.wait_ge(probs_ready, 1)
            for e in range(E0):
                last = mm(ps[:, 5 + e // KT, P * (e % KT):P * (e % KT) + P], probs0[:, e:e + 1].to_broadcast([P, P]), ident[:],
                          start=True, stop=True)
            last.then_inc(probs_bc, 1)
            pe.wait_ge(masked_ready, 1)
            t_.transpose(bank(1)[0:E0, 0:P], masked0[:], ident[:]).then_inc(maskedT_ps, 1)
            pe.wait_ge(maskedT_ready, 1)
            pe.wait_ge(ld_b, 32)
            mm(bank(7), masked0T[:], b2_sb[:], start=True, stop=True)

            pe.wait_ge(poly_ready, 1)
            t_.transpose(bank(0)[:, 0:P], poly_a[:, 0], ident[:]).then_inc(poly_ps, 1)
            for k in (1, 2):
                pe.wait_ge(poly_ready, k + 1)
                mm(bank(0)[:, P * k:P * k + P], poly_a[:, 0], poly_a[:, k], start=True, stop=True).then_inc(poly_ps, 1)
            pe.wait_ge(poly_ready, 4)
            mm(bank(0)[0:1, 3 * P:4 * P], ones[:, 0:1], polyT[:], start=True, stop=True).then_inc(poly_ps, 1)
            pe.wait_ge(polyrow_ready, 1)

            with pe.Fori(0, GROUPS) as g:
                pe.wait_ge(tok_ready, 2 * g + 2)
                for k in range(KT):
                    mm(tiles(1)[:, k], xn[:, P * k:P * k + P], hot_tok[:].rearrange("p j t -> p (j t)"), start=True, stop=True)
                t_.transpose(bank(0)[:, 0:P], hot_gate[:].rearrange("p j t -> p (j t)"), ident[:]).then_inc(gather_ps, 1)
                for r in range(CHUNKS0):
                    mm(bank(3 + r), group_rows[:], b1_rows[:, bass.ds(g, 1), D * r:D * r + D].rearrange("p a f -> p (a f)"),
                       start=True, stop=True)
                    pe.wait_ge(exT_ready, g + 1)
                    for k in range(KT):
                        pe.wait_ge(ld_u1[r][k], 16 * (g + 1))
                        for j in range(EG):
                            own = slice(TOP0 * j, TOP0 * j + TOP0)
                            last = mm(bank(3 + r)[own], exT[:, k, own], unit_w1[r][:, k, j], start=False, stop=True,
                                      skip_group_check=True)
                    last.then_inc(mid_ps, 1)
                    pe.wait_ge(mid_ready, CHUNKS0 * g + r + 1)
                    for k in range(KT):
                        last = t_.transpose(tiles(5 + r)[:, k], mid[r][:, P * k:P * k + P], ident[:])
                    last.then_inc(midT_ps, 1)
                    pe.wait_ge(midT_ready, CHUNKS0 * g + r + 1)
                    for k in range(KT):
                        pe.wait_ge(ld_u2[r][k], 16 * (g + 1))
                        for j in range(EG):
                            own = slice(TOP0 * j, TOP0 * j + TOP0)
                            last = mm(bank(2)[own], midT[r][:, k, own], unit_w2[r][:, k, j],
                                      start=(r == 0 and k == 0), stop=(r == CHUNKS0 - 1 and k == KT - 1))
                    last.then_inc(unit_free[r], 1)
                pe.wait_ge(unit_ready, g + 1)
                pe.wait_ge(scatter_ready, g + 1)
                mm(bank(7), scatter[:], unit_out[:], start=False, stop=True, skip_group_check=True).then_inc(ffn0_ps, 1)

            transpose_x(2, 0)
            neighbours(xn, polyT)
            pe.wait_ge(ld_gnn_w, 16)
            pe.wait_ge(ld_l1_rows, 32)
            mm(bank(7), poly_rows[:], gnn_b_row[:], start=True, stop=False)
            pe.wait_ge(ah_ready, 3)
            for k in range(KT):
                last = mm(bank(7), ahT[:, k], gnn_w_sb[:, k], start=False, stop=(k == KT - 1))
            last.then_inc(gnn1_ps, 1)
            project(1, wqkv_sb, lambda part: pe.wait_ge(ld_qkv[part], 16))
            keys_values(1)
            attend(1)
            pe.wait_ge(mix_ready, 2)
            for k in range(KT):
                last = t_.transpose(tiles(0)[:, k], mix[:, P * k:P * k + P], ident[:])
            last.then_inc(mixT_ps, 1)
            pe.wait_ge(ld_wout, 16)
            mm(bank(1), ones[0:1, :], bout_row[:], start=True, stop=False)
            pe.wait_ge(mixT_ready, 1)
            for k in range(KT):
                last = mm(bank(1), mixT[:, k], wout_sb[:, k], start=False, stop=(k == KT - 1))
            last.then_inc(wout_ps, 1)

            transpose_x(3, 4)

            def up(s, stage, i, lo_done, free, done):
                n = even(s.cols[1])
                pe.wait_ge(lo_done, s.g + 1)
                if s.n > 1:
                    pe.wait_ge(free, s.g - 1)
                hi, lo = stage[s.par]
                for k in range(KT):
                    for xT, w in ((xT_hi, hi), (xT_hi, lo), (xT_lo, hi)):
                        last = mm(bank(i + s.par)[:, 0:n], xT[:, k], w[:, k, 0:n], start=(k == 0 and w is hi and xT is xT_hi),
                                  stop=(k == KT - 1 and xT is xT_lo))
                last.then_inc(done, 1)

            def transpose_h(s):
                pe.wait_ge(h_ready, s.g + 1)
                if s.n > 1:
                    pe.wait_ge(hT_lo_ready, s.g - 1)
                for k in range(s.tiles):
                    rows = min(P, s.cols[1] - P * k)
                    last = t_.transpose(tiles(4 + s.par)[0:rows, k], h[s.par][:, P * k:P * k + rows], ident[:])
                last.then_inc(hT_ps, 1)

            def down(s):
                pe.wait_ge(hT_lo_ready, s.g + 1)
                pe.wait_ge(s3_lo, s.g + 1)
                (h_hi, h_lo), (w_hi, w_lo) = hT[s.par], s3[s.par]
                for k in range(s.tiles):
                    rows = min(P, s.cols[1] - P * k)
                    for a, w in ((h_hi, w_hi), (h_hi, w_lo), (h_lo, w_hi)):
                        last = mm(bank(6), a[0:rows, k], w[0:rows, k],
                                  start=(s.first and k == 0 and a is h_hi and w is w_hi),
                                  stop=(s.last and k == s.tiles - 1 and a is h_lo))
                last.then_inc(down_done, 1)

            def chunk(n, i=None):
                s = Step(n, i)
                up(s, s1, 0, s1_lo, act_ready, a_done)
                if n > 0:
                    transpose_h(Step(n - 1, i))
                up(s, s2, 2, s2_lo, h_ready, b_done)
                if n > 0:
                    down(Step(n - 1, i))

            pe.wait_ge(x_lo_ready, 1)
            for n in range(NC):
                chunk(n)
                if n == 0:
                    pe.wait_ge(xnT_ready, 4)
                    for k in range(KT):
                        mm(bank(7)[:, 0:E1], xnT[:, k], gate1_w[:, k], start=(k == 0), stop=False)
                    mm(bank(7)[:, 0:E1], ones[0:1, :], gate1_b[:], start=False, stop=True).then_inc(gate1_ps, 1)
            with pe.Fori(0, E1 // 2) as i:
                for n in range(NC, 3 * NC):
                    chunk(n, i)
            transpose_h(Step(G_ALL - 1))
            down(Step(G_ALL - 1))


class Step:

    def __init__(self, n, i=None):
        self.n = n
        self.g = n if i is None else 2 * NC * i + n
        self.expert = n // NC if i is None else 2 * i + n // NC
        self.j = n % NC
        self.par = n % 2
        self.cols = CHUNK[self.j]
        self.full, self.rest = self.cols[1] // P, self.cols[1] % P
        self.tiles = self.full + (self.rest > 0)
        self.t0 = self.cols[0] // P
        self.first = i is None and n == 0
        self.last = i is None and n == G_ALL - 1


_INS = ["x", "src", "dst", "edge_weight", "L0_gnn_W_gcn", "L0_gnn_b_gcn", "L0_gnn_W_mlp", "L0_gnn_b_mlp",
        "L0_mix_Wq", "L0_mix_Wkv", "L0_ffn_Wg", "L0_ffn_W1", "L0_ffn_b1", "L0_ffn_W2", "L0_ffn_b2", "L1_gnn_W",
        "L1_gnn_b", "L1_gnn_diffusion_weights", "L1_mix_W_qkv", "L1_mix_W_out", "L1_mix_b_out", "L1_ffn_gate_w",
        "L1_ffn_routing_bias", "L1_ffn_w1", "L1_ffn_w2", "L1_ffn_w3", "L1_ffn_sw1", "L1_ffn_sw2", "L1_ffn_sw3"]


def kernel(**inputs):
    import concourse.bacc as bacc
    from concourse.bass_utils import run_bass_kernel_spmd

    nc = bacc.Bacc("TRN2", target_bir_lowering=False, num_devices=1)
    arrays, args = {}, []
    for name in _INS:
        a = np.ascontiguousarray(inputs[name])
        arrays[f"in_{name}"] = a
        args.append(nc.dram_tensor(f"in_{name}", a.shape, mybir.dt.from_np(a.dtype), kind="ExternalInput").ap())
    args.append(nc.dram_tensor("out_x", (P, D), F32, kind="ExternalOutput").ap())
    gps_kernel(nc, *args)
    r = run_bass_kernel_spmd(nc, [arrays], core_ids=[0])
    return r.results[0]["out_x"]
```

```python
import numpy as np

import concourse.bass as bass
from concourse import mybir

ALU = mybir.AluOpType
ACT = mybir.ActivationFunctionType
AX_X = mybir.AxisListType.X
F32 = mybir.dt.float32
F32R = mybir.dt.float32r
I32 = mybir.dt.int32

P = 128
D = 512
KT = D // P
EDGES = 2048
ET = EDGES // P
EQ = 4
HEADS = 8
DH = D // HEADS
PAIRS = HEADS // 2
PW = 2 * (DH + 1)
E0 = 8
F0 = 1024
TOP0 = max(P * 2 // E0, 1)
EG = P // TOP0
GROUPS = E0 // EG
CHUNKS0 = F0 // D
E1 = 16
K1 = 4
F1 = 1365
CHUNK = [(0, 512), (512, 512), (1024, F1 - 1024)]
NC = len(CHUNK)
G_ALL = NC * (E1 + 1)
SPLIT3 = NC - 1
LN_EPS = 1e-5
ATT_EPS = 1e-6
LEAK = 0.01
TINY = 1e-37


def even(n):
    return n + n % 2


def up32(n):
    return -(-n // 32) * 32


def gps_kernel(nc, x, src, dst, edge_weight, gcn_w, gcn_b, mlp_w, mlp_b, wq, wkv, wg0, w1_0, b1_0, w2_0, b2_0,
               gnn_w, gnn_b, diffusion, wqkv, wout, bout, gate_w, gate_b, w1, w2, w3, sw1, sw2, sw3, out):
    base = up32(nc.sbuf_base)
    size_a = 2 * EG * KT * D * 4
    at_a = base
    size_raw = 2 * up32(KT * F1 * 4) + (2 * KT + 3) * D * 4
    at_b = at_a + size_a
    size_b = max(size_a, size_raw)
    at_c = at_b + size_b
    size_c = 4 * KT * D * 4
    at_d = at_c + size_c

    def place(name, shape, dt, at):
        return nc.alloc_sbuf_tensor_at(name, shape, dt, offset=at)

    class Cursor:

        def __init__(self, at):
            self.at = at

        def __call__(self, name, shape, dt=F32):
            t = place(name, shape, dt, self.at)
            self.at += up32(int(np.prod(shape[1:])) * 4)
            return t

    unit_w1 = [place("unit_w1_a", [P, KT, EG, D], F32, at_a), place("unit_w1_b", [P, KT, EG, D], F32, at_b)]
    unit_w2 = [place("unit_w2_a", [P, KT, EG, D], F32, at_a + size_a // 2),
               place("unit_w2_b", [P, KT, EG, D], F32, at_b + size_a // 2)]
    c = Cursor(at_a + size_a // 2)
    hot_src = [c(f"hot_src{i}", [P, EQ, P], F32R) for i in range(2)]
    hot_dst = [c(f"hot_dst{i}", [P, EQ, 3, P], F32R) for i in range(2)]
    c = Cursor(at_b)
    wq_raw = c("wq_raw", [P, KT, D])
    wkv_raw = c("wkv_raw", [P, 2 * KT, D])
    gcn_w_sb, mlp_w_sb = [], []
    for i in range(2):
        gcn_w_sb.append(c(f"gcn_w_sb{i}", [P, KT, D]))
        mlp_w_sb.append(c(f"mlp_w_sb{i}", [P, KT, D]))
    c = Cursor(at_b)
    w1_raw = c("w1_raw", [P, KT, F1])
    w2_raw = c("w2_raw", [P, KT, F1])
    w3_raw = c("w3_raw", [P, 2 * KT + 3, D])
    c = Cursor(at_c)
    wT_sb = c("wT_sb", [P, KT, 3 * D])
    gcn_b_row = c("gcn_b_row", [1, 2, D])
    mlp_b_row = c("mlp_b_row", [1, 2, D])
    c = Cursor(at_c)
    wk_sb = c("wk_sb", [P, KT, D])
    wv_sb = c("wv_sb", [P, KT, D])
    gnn_w_sb = c("gnn_w_sb", [P, KT, D])
    l1_rows = Cursor(c.at)
    b1_rows = c("b1_rows", [EG, GROUPS, F0])
    gnn_b_row = l1_rows("gnn_b_row", [1, D])
    bout_row = l1_rows("bout_row", [1, D])
    c = Cursor(at_a)
    s1 = [[c("s1_hi0", [P, KT, D], F32R), c("s1_lo0", [P, KT, D], F32R)]]
    s2 = [[c("s2_hi0", [P, KT, D], F32R), c("s2_lo0", [P, KT, D], F32R)]]
    s3 = [[c("s3_hi0", [P, KT, D], F32R), c("s3_lo0", [P, KT, D], F32R)]]
    w = Cursor(c.at)
    s3.append([c("s3_hi1", [P, KT, D], F32R), c("s3_lo1", [P, KT, D], F32R)])
    wq_sb = w("wq_sb", [P, KT, D])
    wout_sb = w("wout_sb", [P, KT, D])
    c = Cursor(at_c)
    s1.append([c("s1_hi1", [P, KT, D], F32R), c("s1_lo1", [P, KT, D], F32R)])
    s2.append([c("s2_hi1", [P, KT, D], F32R), c("s2_lo1", [P, KT, D], F32R)])
    d = Cursor(at_d)
    x0 = d("x0", [P, D])
    x1 = d("x1", [P, D])
    x2 = d("x2", [P, D])
    x3 = x0
    xn = d("xn", [P, D])
    xnT = d("xnT", [P, KT, P])
    xT_hi = d("xT_hi", [P, KT, P], F32R)
    xT_lo = d("xT_lo", [P, KT, P], F32R)
    ident = d("ident", [P, P])
    iota = d("iota", [P, P])
    ones = d("ones", [P, P])
    below = d("below", [P, P])
    below16 = d("below16", [P, E1, E1])
    group_rows = d("group_rows", [EG, P])
    neg_half = d("neg_half", [P, 1])
    adjT = d("adjT", [P, P])
    adj1 = d("adj1", [P, P])
    polyT = d("polyT", [P, P])
    poly_rows = d("poly_rows", [1, P])
    gate0_w = d("gate0_w", [P, KT, E0])
    gate1_w = d("gate1_w", [P, KT, E1])
    gate1_b = d("gate1_b", [1, E1])
    diff_w = d("diff_w", [P, 4])
    src_i = d("src_i", [P, ET], I32)
    dst_i = d("dst_i", [P, ET], I32)
    src_f = d("src_f", [P, ET])
    dst_f = d("dst_f", [P, ET])
    ew = d("ew", [P, ET])
    ew_hi = d("ew_hi", [P, ET], F32R)
    ew_lo = d("ew_lo", [P, ET], F32R)
    stats = d("stats", [P, 6])
    mean_var = d("mean_var", [P, 2])
    var_eps = d("var_eps", [P, 1])
    rstd = d("rstd", [P, 1])
    deg = d("deg", [P, 4])
    probs0 = d("probs0", [P, E0])
    rank0 = d("rank0", [P, EG])
    small = d("small", [P, 8])
    logits1 = d("logits1", [P, E1])
    rank1 = d("rank1", [P, E1])
    weights1 = d("weights1", [P, 1 + E1])
    recip = d("recip", [P, HEADS])
    rank_t = [d(f"rank_t{i}", [P, E1, E1]) for i in range(2)]
    at_e = d.at
    h = [d(f"h{i}", [P, D]) for i in range(2)]
    act_a = [d(f"act_a{i}", [P, D]) for i in range(2)]
    hT_32 = d("hT_32", [P, 3, P])
    hT = [[d(f"hT_hi{i}", [P, KT, P], F32R), d(f"hT_lo{i}", [P, KT, P], F32R)] for i in range(2)]
    e = Cursor(at_e)
    q_phi = e("q_phi", [P, PAIRS, P])
    k_phi = e("k_phi", [P, D])
    v_aug = e("v_aug", [P, HEADS, DH + 1])
    kv_diag = e("kv_diag", [P, PAIRS, PW])
    neg_q = e("neg_q", [P, D])
    neg_k = e("neg_k", [P, D])
    mix = neg_k
    ahT = e("ahT", [P, KT, P])
    gcnT = e("gcnT", [P, KT, P])
    mixT = gcnT
    leak = neg_q
    gnn = e("gnn", [P, D])
    poly_a = e("poly_a", [P, 3, P])
    cnt = e("cnt", [P, 2, P])
    f = Cursor(at_e)
    b2_rows = f("b2_rows", [EG, GROUPS, D])
    rank_diff = f("rank_diff", [P, EG, P])
    rank_ge = f("rank_ge", [P, EG, P])
    hot_tok = f("hot_tok", [P, EG, TOP0])
    hot_gate = f("hot_gate", [P, EG, TOP0])
    scatter = f("scatter", [P, P])
    exT = f("exT", [P, KT, P])
    mid = f("mid", [P, D])
    midT = f("midT", [P, KT, P])
    unit_out = f("unit_out", [P, D])
    assert max(d.at, e.at, f.at) <= nc.sbuf_usable_end, (d.at, e.at)

    ps = nc.alloc_psum_tensor("ps", [P, 8, 512], F32)

    def bank(i):
        return ps[:, i, :]

    def tiles(i):
        return ps[:, i, :].rearrange("p (t n) -> p t n", t=KT)

    def poly_bank(k):
        return bank(6 - k % 2)[:, 3 * P:4 * P]

    def sem(name):
        return nc.alloc_semaphore(name)

    ld_x, ld_edges, ld_small, ld_rows = sem("ld_x"), sem("ld_edges"), sem("ld_small"), sem("ld_rows")
    ld_wq = sem("ld_wq")
    ld_wkv = [sem(f"ld_wkv{i}") for i in range(2)]
    ld_gcn = [sem(f"ld_gcn{i}") for i in range(2)]
    ld_mlp = [sem(f"ld_mlp{i}") for i in range(2)]
    ld_b = sem("ld_b")
    ld_u1 = [[sem(f"ld_u1_{r}{t}") for t in range(KT)] for r in range(2)]
    ld_u2 = [[sem(f"ld_u2_{r}{t}") for t in range(KT)] for r in range(2)]
    ld_gnn_w, ld_wout, ld_l1_rows = sem("ld_gnn_w"), sem("ld_wout"), sem("ld_l1_rows")
    ld_qkv = [sem(f"ld_{i}1") for i in ("q", "k", "v")]
    ld_w1 = [sem(f"ld_w1_{i}") for i in range(NC)]
    ld_w2 = [sem(f"ld_w2_{i}") for i in range(NC)]
    ld_w3 = [sem(f"ld_w3_{i}") for i in range(NC)]
    consts = sem("consts")
    pool_seq = sem("pool_seq")
    seq = sem("seq")
    var_ready, rstd_ready = sem("var_ready"), sem("rstd_ready")
    deg_ready, dinv_ready = sem("deg_ready"), sem("dinv_ready")
    xn_ready, xnT_ps, xnT_ready = sem("xn_ready"), sem("xnT_ps"), sem("xnT_ready")
    hot_ready, hot_used = sem("hot_ready"), sem("hot_used")
    adj1_ready, adjT_ps, adjT_ready = sem("adj1_ready"), sem("adjT_ps"), sem("adjT_ready")
    wT_ps, wT_ready = sem("wT_ps"), sem("wT_ready")
    q_ps, k_ps, v_ps = sem("q_ps"), sem("k_ps"), sem("v_ps")
    negq_ready, negk_ready, expq_ready, expk_ready = (sem(n) for n in ("negq_ready", "negk_ready", "expq_ready", "expk_ready"))
    qphi_ready, kphi_ready, v_ready = sem("qphi_ready"), sem("kphi_ready"), sem("v_ready")
    kv_ps, kv_ready, att_ps, mix_ready = sem("kv_ps"), sem("kv_ready"), sem("att_ps"), sem("mix_ready")
    ah_ps, ah_ready, gcn_ps, gcn_ready = sem("ah_ps"), sem("ah_ready"), sem("gcn_ps"), sem("gcn_ready")
    mlp_ps, leak_ready, gnn_ready = sem("mlp_ps"), sem("leak_ready"), sem("gnn_ready")
    gate0_ps, max0_ready, exp0_ready, probs_ready = sem("gate0_ps"), sem("max0_ready"), sem("exp0_ready"), sem("probs_ready")
    probs_bc, rank_seq = sem("probs_bc"), sem("rank_seq")
    poly_ps, poly_ready, polyrow_ready = sem("poly_ps"), sem("poly_ready"), sem("polyrow_ready")
    tok_ready, hot_gate_ready, gather_ps, exT_ready = sem("tok_ready"), sem("hot_gate_ready"), sem("gather_ps"), sem("exT_ready")
    gateT_ps, scatter_ready = sem("gateT_ps"), sem("scatter_ready")
    mid_ready, midT_ps, midT_ready = sem("mid_ready"), sem("midT_ps"), sem("midT_ready")
    w1_used = [sem(f"w1_used_{r}") for r in "ab"]
    w2_used = [sem(f"w2_used_{r}") for r in "ab"]
    unit_ready, ffn0_ps = sem("unit_ready"), sem("ffn0_ps")
    gnn1_ps, mixT_ps, mixT_ready, wout_ps = sem("gnn1_ps"), sem("mixT_ps"), sem("mixT_ready"), sem("wout_ps")
    x_hi_ready, x_lo_ready = sem("x_hi_ready"), sem("x_lo_ready")
    gate1_ps, negmax1_ready, exp1_ready, weights_ready = sem("gate1_ps"), sem("negmax1_ready"), sem("exp1_ready"), sem("weights_ready")
    s1_hi, s1_lo, s2_hi, s2_lo, s3_hi, s3_lo = (sem(n) for n in ("s1_hi", "s1_lo", "s2_hi", "s2_lo", "s3_hi", "s3_lo"))
    a_done, b_done, act_ready, h_ready = sem("a_done"), sem("b_done"), sem("act_ready"), sem("h_ready")
    hT_ps, hT_hi_ready, hT_lo_ready, down_done = sem("hT_ps"), sem("hT_hi_ready"), sem("hT_lo_ready"), sem("down_done")
    out_ready, out_stored = sem("out_ready"), sem("out_stored")
    N_CONSTS = 7
    RANK_STEPS = 4

    def by_tile(w):
        return w.rearrange("(t p) n -> p t n", p=P)

    def row(v):
        return v.rearrange("(a n) -> a n", a=1)

    w1_0_v = w1_0.rearrange("e (t p) f -> t p e f", p=P)
    w2_0_v = w2_0.rearrange("e (t p) h -> t p e h", p=P)

    block = nc.Block()
    with block as blk:
        @blk.sync
        def _(sp):
            for t, v in ((src_i, src), (dst_i, dst), (ew, edge_weight)):
                sp.dma_start(t[:], v.rearrange("(p t) -> p t", t=ET)).then_inc(ld_edges, 16)
            sp.dma_start(x0[:], x).then_inc(ld_x, 16)
            sp.dma_start(wq_raw[:], by_tile(wq)).then_inc(ld_wq, 16)
            for half in range(2):
                sp.dma_start(wkv_raw[:, KT * half:KT * half + KT], by_tile(wkv[D * half:D * half + D])).then_inc(ld_wkv[half], 16)
            for i in range(2):
                sp.dma_start(gcn_w_sb[i][:], by_tile(gcn_w[i])).then_inc(ld_gcn[i], 16)
                sp.dma_start(mlp_w_sb[i][:], by_tile(mlp_w[i])).then_inc(ld_mlp[i], 16)

            def load_w1(g, r, t):
                sp.dma_start(unit_w1[r][:, t], w1_0_v[t, :, bass.ds(EG * g, EG), D * r:D * r + D]).then_inc(ld_u1[r][t], 16)

            def load_w2(g, r, t):
                sp.dma_start(unit_w2[r][:, t], w2_0_v[KT * r + t, :, bass.ds(EG * g, EG), :]).then_inc(ld_u2[r][t], 16)

            for t in range(KT):
                load_w1(0, 0, t)
            sp.wait_ge(hot_used, ET // EQ)
            for t in range(KT):
                load_w2(0, 0, t)
            sp.wait_ge(wT_ps, 3 * KT)
            for t in range(KT - 1):
                load_w1(0, 1, t)
            sp.wait_ge(gcn_ps, 1)
            load_w1(0, 1, KT - 1)
            sp.wait_ge(mlp_ps, 1)
            load_w2(0, 1, 0)
            sp.wait_ge(gcn_ps, 2)
            load_w2(0, 1, 1)
            sp.wait_ge(mlp_ps, 2)
            sp.dma_start(b1_rows[:], b1_0.rearrange("(g j) f -> j g f", j=EG)).then_inc(ld_b, 16)
            sp.dma_start(b2_rows[:], b2_0.rearrange("(g j) h -> j g h", j=EG)).then_inc(ld_b, 16)
            for t in range(2, KT):
                load_w2(0, 1, t)
            sp.wait_ge(v_ps, 1)
            sp.dma_start(gnn_w_sb[:], by_tile(gnn_w)).then_inc(ld_gnn_w, 16)

            def load_qkv(i, dst):
                sp.dma_start(dst[:], by_tile(wqkv[:, D * i:D * i + D])).then_inc(ld_qkv[i], 16)

            load_qkv(1, wk_sb)
            load_qkv(2, wv_sb)
            with sp.Fori(1, GROUPS) as g:
                for r in range(CHUNKS0):
                    for t in range(KT):
                        sp.wait_ge(w1_used[r], KT * g - KT + t + 1)
                        load_w1(g, r, t)
                    for t in range(KT):
                        sp.wait_ge(w2_used[r], KT * g - KT + t + 1)
                        load_w2(g, r, t)

            sp.wait_ge(w2_used[0], KT * GROUPS)
            load_qkv(0, wq_sb)
            sp.dma_start(wout_sb[:], by_tile(wout)).then_inc(ld_wout, 16)
            sp.wait_ge(w1_used[1], KT * GROUPS)
            sp.dma_start(gnn_b_row[:], row(gnn_b)).then_inc(ld_l1_rows, 16)
            sp.dma_start(bout_row[:], row(bout)).then_inc(ld_l1_rows, 16)

            def load_up(dst, w, j, s):
                c0, n = CHUNK[j]
                sp.dma_start(dst[:, :, c0:c0 + n], by_tile(w)[:, :, c0:c0 + n]).then_inc(s[j], 16)

            def load_down(w, j):
                c0, n = CHUNK[j]
                full, rest = n // P, n % P
                sp.dma_start(w3_raw[:, c0 // P:c0 // P + full], by_tile(w[c0:c0 + full * P, :])).then_inc(ld_w3[j], 16)
                if rest:
                    lo, most = c0 + full * P, rest // 16 * 16
                    sp.dma_start(w3_raw[0:most, c0 // P + full], w[lo:lo + most, :]).then_inc(ld_w3[j], 16)
                    sp.dma_start(w3_raw[most:rest, c0 // P + full], w[lo + most:lo + rest, :]).then_inc(ld_w3[j], 16)

            sp.wait_ge(w2_used[1], KT * GROUPS)
            for j in range(NC):
                load_up(w1_raw, sw1, j, ld_w1)
                load_up(w2_raw, sw2, j, ld_w2)
                load_down(sw3, j)

            def one(w, i):
                return w[bass.ds(i, 1)].rearrange("a r n -> (a r) n")

            with sp.Fori(0, E1) as i:
                for j in range(NC):
                    sp.wait_ge(s1_lo, NC * i + j + 1)
                    load_up(w1_raw, one(w1, i), j, ld_w1)
                    sp.wait_ge(s2_lo, NC * i + j + 1)
                    load_up(w2_raw, one(w2, i), j, ld_w2)
                    if j == NC - 1:
                        sp.wait_ge(down_done, NC * i + j + 1)
                    else:
                        sp.wait_ge(s3_lo, SPLIT3 * i + j + 1)
                    load_down(one(w3, i), j)
            sp.wait_ge(out_ready, 1)
            sp.dma_start(out, xn[:]).then_inc(out_stored, 16)
            sp.wait_ge(out_stored, 16)

        @blk.gpsimd
        def _(pool):
            pg = nc.gpsimd
            n = [0]

            def then(ins):
                n[0] += 1
                ins.then_inc(pool_seq, 1)
                pool.wait_ge(pool_seq, n[0])

            pg.iota(iota[:], [[1, P]], base=0, channel_multiplier=0, allow_small_or_imprecise_dtypes=True).then_inc(consts, 1)
            pg.memset(neg_half[:], -0.5).then_inc(consts, 1)
            then(pg.memset(ident[:], 0.0))
            pg.affine_select(out=ident[:], in_=ident[:], compare_op=ALU.not_equal, fill=1.0, base=0,
                             pattern=[[-1, P]], channel_multiplier=1).then_inc(consts, 1)
            pg.memset(ones[:], 1.0).then_inc(consts, 1)
            then(pg.memset(below[:], 1.0))
            pg.affine_select(out=below[:], in_=below[:], compare_op=ALU.is_gt, fill=0.0, base=0,
                             pattern=[[-1, P]], channel_multiplier=1).then_inc(consts, 1)
            then(pg.memset(below16[:], 1.0))
            pg.affine_select(out=below16[:], in_=below16[:], compare_op=ALU.is_gt, fill=0.0, base=0,
                             pattern=[[1, E1], [-1, E1]], channel_multiplier=0).then_inc(consts, 1)
            then(pg.memset(group_rows[:], 0.0))
            v = group_rows[:].rearrange("p (j t) -> p j t", j=EG)
            pg.affine_select(out=v, in_=v, compare_op=ALU.not_equal, fill=1.0, base=0,
                             pattern=[[-1, EG], [0, TOP0]], channel_multiplier=1).then_inc(consts, 1)

            def rsqrt_var(l):
                pool.wait_ge(var_ready, l + 1)
                pg.tensor_tensor(rstd[:], var_eps[:], neg_half[:], ALU.pow).then_inc(rstd_ready, 1)

            pool.wait_ge(consts, 2)
            rsqrt_var(0)
            pool.wait_ge(deg_ready, 1)
            pg.tensor_tensor(deg[:, 1:2], deg[:, 0:1], neg_half[:], ALU.pow).then_inc(dinv_ready, 1)
            for l in range(1, 4):
                rsqrt_var(l)

        @blk.scalar
        def _(act):
            a = nc.scalar
            act.dma_start(gcn_b_row[:], gcn_b.rearrange("(a l) n -> a l n", a=1)).then_inc(ld_rows, 16)
            act.dma_start(mlp_b_row[:], mlp_b.rearrange("(a l) n -> a l n", a=1)).then_inc(ld_rows, 16)
            act.dma_start(gate0_w[:], by_tile(wg0)).then_inc(ld_small, 16)
            act.dma_start(gate1_w[:], by_tile(gate_w)).then_inc(ld_small, 16)
            act.dma_start(gate1_b[:], row(gate_b)).then_inc(ld_small, 16)
            act.dma_start(diff_w[:], row(diffusion).to_broadcast([P, 4])).then_inc(ld_small, 16)

            def copy_wT(i):
                act.wait_ge(wT_ps, i + 1)
                a.copy(wT_sb[:, i % KT, D * (i // KT):D * (i // KT) + D], bank(2 + i % 2)).then_inc(wT_ready, 1)

            def exp_q(l):
                act.wait_ge(negq_ready, l + 1)
                a.activation(neg_q[:], neg_q[:], ACT.Exp).then_inc(expq_ready, 1)

            def exp_k(l):
                act.wait_ge(negk_ready, l + 1)
                a.activation(neg_k[:], neg_k[:], ACT.Exp).then_inc(expk_ready, 1)

            def copy_v(l):
                act.wait_ge(v_ps, l + 1)
                a.copy(v_aug[:, :, 0:DH], bank(4).rearrange("p (h v) -> p h v", h=HEADS)).then_inc(v_ready, 1)

            def copy_ah(i):
                act.wait_ge(ah_ps, i + 1)
                a.copy(ahT[:], tiles(1)).then_inc(ah_ready, 1)

            def copy_gcn(layer):
                act.wait_ge(gcn_ps, layer + 1)
                a.copy(gcnT[:], tiles(7)).then_inc(gcn_ready, 1)

            def leaked(layer):
                act.wait_ge(mlp_ps, layer + 1)
                if layer == 0:
                    act.wait_ge(qphi_ready, 1)
                else:
                    act.wait_ge(gnn_ready, 1)
                a.mul(leak[:], bank(0), LEAK).then_inc(leak_ready, 1)

            for i in range(KT):
                copy_wT(i)
            act.wait_ge(xnT_ps, 1)
            a.copy(xnT[:], tiles(0)).then_inc(xnT_ready, 1)
            for i in range(KT, 3 * KT):
                copy_wT(i)
            copy_ah(0)
            exp_q(0)
            exp_k(0)
            copy_gcn(0)
            leaked(0)
            copy_v(0)
            copy_ah(1)
            copy_gcn(1)
            leaked(1)

            act.wait_ge(max0_ready, 1)
            a.activation(probs0[:], bank(1)[:, 0:E0], ACT.Exp, bias=small[:, 0:1],
                         accum_out=small[:, 1:2]).then_inc(exp0_ready, 1)

            with act.Fori(0, GROUPS) as g:
                act.wait_ge(gather_ps, g + 1)
                a.copy(exT[:], tiles(1)).then_inc(exT_ready, 1)
                for r in range(CHUNKS0):
                    act.wait_ge(w1_used[r], KT * g + KT)
                    a.activation(mid[:], bank(3 + r), ACT.Gelu).then_inc(mid_ready, 1)
                act.wait_ge(w2_used[1], KT * g + KT)
                a.copy(unit_out[:], bank(2)).then_inc(unit_ready, 1)

            def up_hi(s, raw, landed, stage, used, done):
                c0, n = s.cols
                act.wait_ge(landed[s.j], 16 * (s.expert + 1))
                if s.n > 1:
                    act.wait_ge(used, s.g - 1)
                a.copy(stage[s.par][0][:, :, 0:n], raw[:, :, c0:c0 + n]).then_inc(done, 1)

            def down_hi(s):
                if s.whole:
                    return
                act.wait_ge(ld_w3[s.j], 16 * (s.expert + 1))
                if s.n > 1:
                    act.wait_ge(down_done, s.g - 1)
                a.copy(s3[s.par][0][:], w3_raw[:, s.t0:s.t0 + KT]).then_inc(s3_hi, 1)

            def silu(s):
                act.wait_ge(a_done, s.g + 1)
                if s.n > 1:
                    act.wait_ge(h_ready, s.g - 1)
                n = s.cols[1]
                a.activation(act_a[s.par][:, 0:n], bank(s.par)[:, 0:n], ACT.Silu).then_inc(act_ready, 1)

            def hT_hi(s):
                act.wait_ge(hT_ps, s.g + 1)
                if s.whole:
                    a.copy(hT_32[:, 0:s.full], tiles(4 + s.par)[:, 0:s.full])
                    a.copy(hT_32[0:s.rest, s.full], tiles(4 + s.par)[0:s.rest, s.full]).then_inc(hT_hi_ready, 1)
                else:
                    a.copy(hT[s.par][0][:], tiles(4 + s.par)).then_inc(hT_hi_ready, 1)

            def chunk(n, i=None):
                s = Step(n, i)
                if n > 1 and not s.last:
                    up_hi(s, w1_raw, ld_w1, s1, a_done, s1_hi)
                if n > 1:
                    hT_hi(Step(n - 2, i))
                if n > 1 and not s.last:
                    up_hi(s, w2_raw, ld_w2, s2, b_done, s2_hi)
                if n == 1:
                    act.wait_ge(negmax1_ready, 1)
                    a.activation(weights1[:, 1:1 + E1], logits1[:], ACT.Exp, bias=small[:, 0:1]).then_inc(exp1_ready, 1)
                silu(Step(n - 1, i))
                if n > 1:
                    down_hi(Step(n - 1, i))

            copy_ah(2)
            act.wait_ge(ffn0_ps, GROUPS)
            up_hi(Step(0), w1_raw, ld_w1, s1, a_done, s1_hi)
            exp_k(1)
            up_hi(Step(0), w2_raw, ld_w2, s2, b_done, s2_hi)
            copy_v(1)
            exp_q(1)
            down_hi(Step(0))
            act.wait_ge(gnn1_ps, 1)
            up_hi(Step(1), w1_raw, ld_w1, s1, a_done, s1_hi)
            up_hi(Step(1), w2_raw, ld_w2, s2, b_done, s2_hi)
            act.wait_ge(xnT_ps, 4)
            a.copy(xT_hi[:], tiles(4)).then_inc(x_hi_ready, 1)
            for n in range(1, NC):
                chunk(n)
            with act.Fori(0, E1 // 2 - 1) as i:
                for n in range(NC, 3 * NC):
                    chunk(n, i)
            for n in range(NC, 3 * NC):
                chunk(n, E1 // 2 - 1)
            hT_hi(Step(G_ALL - 2))
            silu(Step(G_ALL - 1))
            hT_hi(Step(G_ALL - 1))

        @blk.vector
        def _(dve):
            v = nc.vector
            n_seq = [0]

            def then(ins):
                n_seq[0] += 1
                ins.then_inc(seq, 1)
                dve.wait_ge(seq, n_seq[0])

            def variance(x_in):
                then(v.bn_stats(stats[:], x_in[:]))
                then(v.bn_aggr(mean_var[:], stats[:]))
                v.tensor_scalar(var_eps[:], mean_var[:, 1:2], LN_EPS, None, ALU.add).then_inc(var_ready, 1)

            def normalise(l, x_in):
                dve.wait_ge(rstd_ready, l + 1)
                v.tensor_scalar(xn[:], x_in[:], mean_var[:, 0:1], rstd[:], ALU.subtract, ALU.mult).then_inc(xn_ready, 1)

            def layernorm(l, x_in):
                variance(x_in)
                normalise(l, x_in)

            def copy_xnT(l, i):
                dve.wait_ge(xnT_ps, l + 1)
                v.tensor_copy(xnT[:], tiles(i)).then_inc(xnT_ready, 1)

            def negative(ready, i, neg, done):
                dve.wait_ge(*ready)
                v.tensor_scalar(neg[:], bank(i), 0.0, None, ALU.min).then_inc(done, 1)

            def phi(z, ready, i, neg, done):
                dve.wait_ge(*ready)
                v.scalar_tensor_tensor(z, bank(i), 0.0, neg[:], ALU.max, ALU.add).then_inc(done, 1)

            def negative_q(l):
                negative((q_ps, l + 1), 2, neg_q, negq_ready)

            def phi_q(l):
                phi(q_phi[:].rearrange("p a n -> p (a n)"), (expq_ready, l + 1), 2, neg_q, qphi_ready)

            def negative_k(l):
                negative((k_ps, l + 1), 3, neg_k, negk_ready)

            def phi_k(l):
                phi(k_phi[:], (expk_ready, l + 1), 3, neg_k, kphi_ready)

            def keep_diagonal(l):
                dve.wait_ge(kv_ps, l + 1)
                kv = ps[:, 5:7, 0:2 * PW].rearrange("p b (i c) -> p b i c", i=2)
                own = kv_diag[:].rearrange("p (b i) c -> p b i c", i=2)
                for half in range(2):
                    rows, cols = slice(DH * half, DH * half + DH), slice(PW // 2 * half, PW // 2 * half + PW // 2)
                    last = v.tensor_copy(own[rows, :, :, cols], kv[rows, :, :, cols])
                last.then_inc(kv_ready, 1)

            def attended(l):
                dve.wait_ge(att_ps, l + 1)
                o = ps[:, 3:5, 0:2 * PW].rearrange("p b (h c) -> p b h c", h=HEADS // 2)
                r = recip[:].rearrange("p (b h) -> p b h", b=2)
                then(v.tensor_scalar(r, o[:, :, :, DH], ATT_EPS, None, ALU.add))
                then(v.reciprocal(recip[:], recip[:]))
                v.tensor_tensor(mix[:].rearrange("p (b h c) -> p b h c", b=2, c=DH), o[:, :, :, 0:DH],
                                r.unsqueeze(3).to_broadcast([P, 2, HEADS // 2, DH]), ALU.mult).then_inc(mix_ready, 1)

            def leaky(layer):
                dve.wait_ge(leak_ready, layer + 1)
                v.tensor_tensor(gnn[:], bank(0), leak[:], ALU.max).then_inc(gnn_ready, 1)

            def up_lo(s, raw, stage, hi_done, done):
                c0, n = s.cols
                dve.wait_ge(hi_done, s.g + 1)
                hi, lo = stage[s.par]
                v.tensor_tensor(lo[:, :, 0:n], raw[:, :, c0:c0 + n], hi[:, :, 0:n].bitcast(F32), ALU.subtract).then_inc(done, 1)

            def down_lo(s):
                if s.whole:
                    return
                dve.wait_ge(s3_hi, s.g3 + 1)
                hi, lo = s3[s.par]
                v.tensor_tensor(lo[:], w3_raw[:, s.t0:s.t0 + KT], hi[:].bitcast(F32), ALU.subtract).then_inc(s3_lo, 1)

            def fill_attention():
                v.memset(kv_diag[:], 0.0)
                v.memset(v_aug[:, :, DH:DH + 1], 1.0)

            fill_attention()
            v.memset(weights1[:, 0:1], 1.0)
            dve.wait_ge(ld_edges, 48)
            v.tensor_copy(src_f[:], src_i[:])
            v.tensor_copy(dst_f[:], dst_i[:])
            then(v.tensor_copy(ew_hi[:], ew[:]))
            then(v.tensor_tensor(ew_lo[:], ew[:], ew_hi[:].bitcast(F32), ALU.subtract))
            dve.wait_ge(consts, N_CONSTS)
            cols = iota[:].unsqueeze(1).to_broadcast([P, EQ, P])
            for q in range(ET // EQ):
                def of_edge(t):
                    return t[:, EQ * q:EQ * q + EQ].bitcast(F32).unsqueeze(2).to_broadcast([P, EQ, P])
                if q > 1:
                    dve.wait_ge(hot_used, q - 1)
                hot = hot_dst[q % 2]
                v.tensor_tensor(hot_src[q % 2][:], cols, of_edge(src_f), ALU.is_equal)
                then(v.tensor_tensor(hot[:, :, 2], cols, of_edge(dst_f), ALU.is_equal))
                v.tensor_tensor(hot[:, :, 0], hot[:, :, 2].bitcast(F32), of_edge(ew_hi), ALU.mult)
                v.tensor_tensor(hot[:, :, 1], hot[:, :, 2].bitcast(F32), of_edge(ew_lo), ALU.mult).then_inc(hot_ready, 1)
                if q == 0:
                    dve.wait_ge(ld_x, 16)
                    variance(x0)
                if q == 1:
                    normalise(0, x0)
            dve.wait_ge(hot_used, ET // EQ)
            v.tensor_scalar(cnt[:, 0], bank(7)[:, 2 * P:3 * P], 1.0, None, ALU.min)
            then(v.tensor_copy(adj1[:], bank(7)[:, 0:P]))
            then(v.tensor_tensor(adj1[:], bank(7)[:, P:2 * P], adj1[:], ALU.add))
            then(v.tensor_reduce(deg[:, 2:3], adj1[:], AX_X, ALU.add))
            v.tensor_scalar(deg[:, 0:1], deg[:, 2:3], TINY, None, ALU.max).then_inc(deg_ready, 1)
            then(v.tensor_scalar(deg[:, 3:4], deg[:, 2:3], 0.0, None, ALU.is_gt))
            dve.wait_ge(dinv_ready, 1)
            then(v.tensor_tensor(deg[:, 2:3], deg[:, 1:2], deg[:, 3:4], ALU.mult))
            v.tensor_scalar(adj1[:], adj1[:], deg[:, 2:3], None, ALU.mult).then_inc(adj1_ready, 1)
            negative_q(0)
            dve.wait_ge(adjT_ps, 1)
            v.tensor_scalar(adjT[:], bank(1)[:, 0:P], deg[:, 2:3], None, ALU.mult)
            v.tensor_tensor(cnt[:, 1], bank(1)[:, P:2 * P], cnt[:, 0], ALU.add).then_inc(adjT_ready, 1)

            def power(k):
                dve.wait_ge(poly_ps, k)
                v.tensor_copy(poly_a[:, k], poly_bank(k)).then_inc(poly_ready, 1)
                dve.wait_ge(poly_ready, k + 1)
                then(v.scalar_tensor_tensor(polyT[:], poly_a[:, k], diff_w[:, k:k + 1], polyT[:], ALU.mult, ALU.add))

            negative_k(0)
            dve.wait_ge(adjT_ready, 1)
            then(v.tensor_scalar(cnt[:, 1], cnt[:, 1], 1.0, None, ALU.min))
            then(v.tensor_tensor(cnt[:, 1], cnt[:, 1], ident[:], ALU.add))
            then(v.tensor_reduce(small[:, 4:5], cnt[:, 1], AX_X, ALU.add))
            then(v.tensor_scalar(small[:, 4:5], small[:, 4:5], 1.0, None, ALU.max))
            then(v.reciprocal(small[:, 5:6], small[:, 4:5]))
            v.tensor_scalar(poly_a[:, 0], cnt[:, 1], small[:, 5:6], None, ALU.mult).then_inc(poly_ready, 1)
            dve.wait_ge(ld_small, 64)
            then(v.tensor_scalar(polyT[:], ident[:], diff_w[:, 0:1], None, ALU.mult))
            phi_q(0)
            phi_k(0)
            power(1)
            leaky(0)
            power(2)
            keep_diagonal(0)
            dve.wait_ge(poly_ps, 3)
            v.scalar_tensor_tensor(polyT[:], poly_bank(3), diff_w[:, 3:4], polyT[:], ALU.mult, ALU.add).then_inc(poly_ready, 1)
            attended(0)
            dve.wait_ge(mix_ready, 1)
            v.tensor_tensor(x1[:], x0[:], mix[:], ALU.add)
            dve.wait_ge(poly_ps, 4)
            v.tensor_copy(poly_rows[:], poly_bank(4)[0:1, :]).then_inc(polyrow_ready, 1)
            leaky(1)
            dve.wait_ge(gnn_ready, 2)
            then(v.tensor_tensor(x1[:], x1[:], gnn[:], ALU.add))

            layernorm(1, x1)
            copy_xnT(1, 0)
            dve.wait_ge(gate0_ps, 1)
            then(v.reduce_max(small[:, 2:3], bank(1)[:, 0:E0], AX_X))
            v.tensor_scalar(small[:, 0:1], small[:, 2:3], -1.0, None, ALU.mult).then_inc(max0_ready, 1)
            dve.wait_ge(exp0_ready, 1)
            then(v.reciprocal(small[:, 3:4], small[:, 1:2]))
            v.tensor_scalar(probs0[:], probs0[:], small[:, 3:4], None, ALU.mult).then_inc(probs_ready, 1)
            dve.wait_ge(probs_bc, 1)

            with dve.Fori(0, GROUPS) as g:
                steps = [0]

                def then_next(ins):
                    steps[0] += 1
                    ins.then_inc(rank_seq, 1)
                    dve.wait_ge(rank_seq, RANK_STEPS * g + steps[0])

                every = ps[:, bass.ds(5 + g, 1), :].rearrange("p b (e m) -> p (b e) m", m=P)
                own = probs0[:, bass.ds(EG * g, EG)]
                then_next(v.tensor_tensor(rank_diff[:], every, own.unsqueeze(2).to_broadcast([P, EG, P]), ALU.subtract))
                then_next(v.scalar_tensor_tensor(rank_ge[:], rank_diff[:], 0.0,
                                                 below[:].unsqueeze(1).to_broadcast([P, EG, P]), ALU.is_ge, ALU.mult))
                then_next(v.scalar_tensor_tensor(rank_ge[:], rank_diff[:], 0.0, rank_ge[:], ALU.is_gt, ALU.max))
                then_next(v.tensor_reduce(rank0[:], rank_ge[:], AX_X, ALU.add))
                v.tensor_tensor(hot_tok[:], iota[:, 0:TOP0].unsqueeze(1).to_broadcast([P, EG, TOP0]),
                                rank0[:].unsqueeze(2).to_broadcast([P, EG, TOP0]), ALU.is_equal).then_inc(tok_ready, 1)
                dve.wait_ge(tok_ready, g + 1)
                v.tensor_tensor(hot_gate[:], hot_tok[:], own.unsqueeze(2).to_broadcast([P, EG, TOP0]),
                                ALU.mult).then_inc(hot_gate_ready, 1)
                dve.wait_ge(gateT_ps, g + 1)
                v.tensor_copy(scatter[:], bank(0)[:, 0:P]).then_inc(scatter_ready, 1)
                for r in range(CHUNKS0):
                    dve.wait_ge(midT_ps, CHUNKS0 * g + r + 1)
                    v.tensor_copy(midT[:], tiles(5)).then_inc(midT_ready, 1)
            dve.wait_ge(ffn0_ps, GROUPS)
            then(v.tensor_copy(x2[:], bank(7)))

            layernorm(2, x2)
            fill_attention()
            copy_xnT(2, 0)
            negative_k(1)
            phi_k(1)
            up_lo(Step(0), w1_raw, s1, s1_hi, s1_lo)
            up_lo(Step(0), w2_raw, s2, s2_hi, s2_lo)
            negative_q(1)
            phi_q(1)
            keep_diagonal(1)
            attended(1)
            dve.wait_ge(gnn1_ps, 1)
            v.scalar_tensor_tensor(x1[:], bank(7), 0.0, x2[:], ALU.max, ALU.add)
            dve.wait_ge(mixT_ps, 1)
            v.tensor_copy(mixT[:], tiles(0)).then_inc(mixT_ready, 1)
            down_lo(Step(0))
            dve.wait_ge(wout_ps, 1)
            then(v.tensor_tensor(x3[:], bank(1), x1[:], ALU.add))
            layernorm(3, x3)

            dve.wait_ge(x_hi_ready, 1)
            v.tensor_tensor(xT_lo[:], tiles(4), xT_hi[:].bitcast(F32), ALU.subtract).then_inc(x_lo_ready, 1)
            copy_xnT(3, 4)

            def gated(s):
                dve.wait_ge(act_ready, s.g + 1)
                dve.wait_ge(b_done, s.g + 1)
                if s.n > 1:
                    dve.wait_ge(hT_ps, s.g - 1)
                n = s.cols[1]
                v.scalar_tensor_tensor(h[s.par][:, 0:n], act_a[s.par][:, 0:n], weights1[:, bass.ds(s.expert, 1)],
                                       bank(2 + s.par)[:, 0:n], ALU.mult, ALU.mult).then_inc(h_ready, 1)

            def hT_lo(s):
                if s.whole:
                    return
                dve.wait_ge(hT_hi_ready, s.g + 1)
                hi, lo = hT[s.par]
                v.tensor_tensor(lo[:], tiles(4 + s.par), hi[:].bitcast(F32), ALU.subtract).then_inc(hT_lo_ready, 1)

            def chunk(n, i=None):
                s = Step(n, i)
                if not s.last:
                    up_lo(s, w1_raw, s1, s1_hi, s1_lo)
                if n == 1:
                    router_max()
                if n == 2:
                    router()
                if n > 1:
                    hT_lo(Step(n - 2, i))
                if not s.last:
                    up_lo(s, w2_raw, s2, s2_hi, s2_lo)
                gated(Step(n - 1, i))
                if n > 1:
                    down_lo(Step(n - 1, i))

            def router_max():
                dve.wait_ge(gate1_ps, 1)
                then(v.tensor_copy(logits1[:], bank(7)[:, 0:E1]))
                then(v.reduce_max(small[:, 2:3], logits1[:], AX_X))
                v.tensor_scalar(small[:, 0:1], small[:, 2:3], -1.0, None, ALU.mult).then_inc(negmax1_ready, 1)

            def router():
                other = logits1[:].unsqueeze(1).to_broadcast([P, E1, E1])
                own = logits1[:].unsqueeze(2).to_broadcast([P, E1, E1])
                v.tensor_tensor(rank_t[0][:], other, own, ALU.is_gt)
                then(v.tensor_tensor(rank_t[1][:], other, own, ALU.is_equal))
                then(v.tensor_tensor(rank_t[1][:], rank_t[1][:], below16[:], ALU.mult))
                then(v.tensor_tensor(rank_t[0][:], rank_t[0][:], rank_t[1][:], ALU.add))
                then(v.tensor_reduce(rank1[:], rank_t[0][:], AX_X, ALU.add))
                dve.wait_ge(exp1_ready, 1)
                w = weights1[:, 1:1 + E1]
                then(v.scalar_tensor_tensor(w, rank1[:], float(K1), w, ALU.is_lt, ALU.mult))
                then(v.tensor_reduce(small[:, 6:7], w, AX_X, ALU.add))
                then(v.reciprocal(small[:, 7:8], small[:, 6:7]))
                then(v.tensor_scalar(w, w, small[:, 7:8], None, ALU.mult))

            for n in range(1, NC):
                chunk(n)
            with dve.Fori(0, E1 // 2 - 1) as i:
                for n in range(NC, 3 * NC):
                    chunk(n, i)
            for n in range(NC, 3 * NC):
                chunk(n, E1 // 2 - 1)
            hT_lo(Step(G_ALL - 2))
            gated(Step(G_ALL - 1))
            dve.wait_ge(down_done, G_ALL)
            v.tensor_tensor(xn[:], bank(6), x3[:], ALU.add).then_inc(out_ready, 1)

        @blk.tensor
        def _(pe):
            t_ = nc.tensor
            mm = t_.matmul

            def transpose_x(l, i):
                pe.wait_ge(xn_ready, l + 1)
                for k in range(KT):
                    last = t_.transpose(tiles(i)[:, k], xn[:, P * k:P * k + P], ident[:])
                last.then_inc(xnT_ps, 1)

            def project_q(w, ms=range(KT)):
                for m in ms:
                    for k in range(KT):
                        last = mm(tiles(2)[:, m], w[:, k, P * m:P * m + P], xnT[:, k], start=(k == 0), stop=(k == KT - 1))
                if KT - 1 in ms:
                    last.then_inc(q_ps, 1)

            def project_kv(i, done, w, ks=range(KT)):
                for k in ks:
                    last = mm(bank(i), xnT[:, k], w[:, k], start=(k == 0), stop=(k == KT - 1))
                if KT - 1 in ks:
                    last.then_inc(done, 1)

            def keys_values(l):
                pe.wait_ge(kphi_ready, l + 1)
                pe.wait_ge(v_ready, l + 1)
                for p in range(PAIRS):
                    last = mm(ps[:, 5 + p // 2, PW * (p % 2):PW * (p % 2) + PW], k_phi[:, P * p:P * p + P],
                              v_aug[:, 2 * p:2 * p + 2].rearrange("p h c -> p (h c)"), start=True, stop=True)
                last.then_inc(kv_ps, 1)

            def attend(l):
                pe.wait_ge(kv_ready, l + 1)
                pe.wait_ge(qphi_ready, l + 1)
                for p in range(PAIRS):
                    last = mm(ps[:, 3 + p // 2, PW * (p % 2):PW * (p % 2) + PW], q_phi[:, p], kv_diag[:, p], start=True, stop=True)
                last.then_inc(att_ps, 1)

            def neighbours(rows, adj):
                for k in range(KT):
                    last = mm(tiles(1)[:, k], rows[:, P * k:P * k + P], adj[:], start=True, stop=True)
                last.then_inc(ah_ps, 1)

            def transpose_w(i):
                part, k = i // KT, i % KT
                if i % (KT) == 0:
                    if part == 0:
                        pe.wait_ge(ld_wq, 16)
                    else:
                        pe.wait_ge(ld_wkv[part - 1], 16)
                if i > 1:
                    pe.wait_ge(wT_ready, i - 1)
                raw, o0 = (wq_raw, 0) if part == 0 else (wkv_raw, KT * (part - 1))
                for o in range(KT):
                    last = t_.transpose(tiles(2 + i % 2)[:, o], raw[:, o0 + o, P * k:P * k + P], ident[:])
                last.then_inc(wT_ps, 1)

            def count_edges(q):
                pe.wait_ge(hot_ready, q + 1)
                for t in range(EQ):
                    last = mm(bank(7)[:, 0:3 * P], hot_src[q % 2][:, t], hot_dst[q % 2][:, t].rearrange("p a n -> p (a n)"),
                              start=(q == 0 and t == 0), stop=(q == ET // EQ - 1 and t == EQ - 1))
                last.then_inc(hot_used, 1)

            def power(k):
                pe.wait_ge(poly_ready, k)
                if k == 1:
                    last = t_.transpose(poly_bank(1), poly_a[:, 0], ident[:])
                elif k < 4:
                    last = mm(poly_bank(k), poly_a[:, 0], poly_a[:, k - 1], start=True, stop=True)
                else:
                    last = mm(poly_bank(4)[0:1, :], ones[:, 0:1], polyT[:], start=True, stop=True)
                last.then_inc(poly_ps, 1)

            def gcn_product(layer):
                pe.wait_ge(ld_rows, 32)
                pe.wait_ge(ld_gcn[layer], 16)
                pe.wait_ge(ah_ready, layer + 1)
                for m in range(KT):
                    mm(tiles(7)[:, m], gcn_b_row[:, layer, P * m:P * m + P], ones[0:1, :], start=True, stop=False)
                    for k in range(KT):
                        last = mm(tiles(7)[:, m], gcn_w_sb[layer][:, k, P * m:P * m + P], ahT[:, k],
                                  start=False, stop=(k == KT - 1))
                last.then_inc(gcn_ps, 1)

            def mlp_product(layer):
                pe.wait_ge(ld_mlp[layer], 16)
                mm(bank(0), ones[0:1, :], mlp_b_row[:, layer], start=True, stop=False)
                pe.wait_ge(gcn_ready, layer + 1)
                for k in range(KT):
                    last = mm(bank(0), gcnT[:, k], mlp_w_sb[layer][:, k], start=False, stop=(k == KT - 1))
                last.then_inc(mlp_ps, 1)

            def keep_warm(steps, i):
                for _ in range(steps):
                    mm(tiles(i), ident[:], ones[:].unsqueeze(1).to_broadcast([P, KT, P]), start=True, stop=True)

            pe.wait_ge(consts, N_CONSTS)
            for i in range(KT):
                transpose_w(i)
            count_edges(0)
            transpose_x(0, 0)
            for i in range(KT, 2 * KT):
                transpose_w(i)
            count_edges(1)
            count_edges(2)
            for i in range(2 * KT, 3 * KT):
                transpose_w(i)

            pe.wait_ge(xnT_ready, 1)
            pe.wait_ge(wT_ready, 3 * KT)
            project_q(wT_sb, range(KT // 2))
            count_edges(3)
            project_q(wT_sb, range(KT // 2, KT))
            wT_k, wT_v = wT_sb[:, :, D:2 * D], wT_sb[:, :, 2 * D:3 * D]
            project_kv(3, k_ps, wT_k, range(1))
            pe.wait_ge(adj1_ready, 1)
            t_.transpose(bank(1)[:, 0:P], adj1[:], ident[:])
            t_.transpose(bank(1)[:, P:2 * P], cnt[:, 0], ident[:]).then_inc(adjT_ps, 1)
            project_kv(3, k_ps, wT_k, range(1, KT))
            pe.wait_ge(adjT_ready, 1)
            neighbours(xn, adjT)
            project_kv(4, v_ps, wT_v, range(1))
            gcn_product(0)
            power(1)
            project_kv(4, v_ps, wT_v, range(1, 2))
            mlp_product(0)
            project_kv(4, v_ps, wT_v, range(2, KT))
            power(2)
            pe.wait_ge(gnn_ready, 1)
            neighbours(gnn, adjT)
            pe.wait_ge(poly_ready, 3)
            keys_values(0)
            gcn_product(1)
            pe.wait_ge(kv_ready, 1)
            power(3)
            attend(0)
            power(4)
            mlp_product(1)
            keep_warm(8, 7)

            transpose_x(1, 0)
            keep_warm(1, 7)
            pe.wait_ge(xnT_ready, 2)
            pe.wait_ge(ld_small, 64)
            for k in range(KT):
                last = mm(bank(1)[:, 0:E0], xnT[:, k], gate0_w[:, k], start=(k == 0), stop=(k == KT - 1))
            last.then_inc(gate0_ps, 1)
            keep_warm(2, 7)
            pe.wait_ge(probs_ready, 1)
            for e in range(E0):
                last = t_.transpose(ps[:, 5 + e // KT, P * (e % KT):P * (e % KT) + P],
                                    probs0[:, e:e + 1].to_broadcast([P, P]), ident[:])
            last.then_inc(probs_bc, 1)
            keep_warm(4, 7)
            mm(bank(7), ident[:], x1[:], start=True, stop=True)
            pe.wait_ge(ld_b, 32)

            with pe.Fori(0, GROUPS) as g:
                for r in range(CHUNKS0):
                    mm(bank(3 + r), group_rows[:], b1_rows[:, bass.ds(g, 1), D * r:D * r + D].rearrange("p a f -> p (a f)"),
                       start=True, stop=True)
                mm(bank(2), group_rows[:], b2_rows[:, bass.ds(g, 1), :].rearrange("p a f -> p (a f)"), start=True, stop=True)
                pe.wait_ge(tok_ready, g + 1)
                for k in range(KT):
                    last = mm(tiles(1)[:, k], xn[:, P * k:P * k + P], hot_tok[:].rearrange("p j t -> p (j t)"), start=True, stop=True)
                last.then_inc(gather_ps, 1)
                pe.wait_ge(hot_gate_ready, g + 1)
                t_.transpose(bank(0)[:, 0:P], hot_gate[:].rearrange("p j t -> p (j t)"), ident[:]).then_inc(gateT_ps, 1)
                pe.wait_ge(exT_ready, g + 1)
                for r in range(CHUNKS0):
                    for k in range(KT):
                        pe.wait_ge(ld_u1[r][k], 16 * (g + 1))
                        for j in range(EG):
                            own = slice(TOP0 * j, TOP0 * j + TOP0)
                            last = mm(bank(3 + r)[own], exT[:, k, own], unit_w1[r][:, k, j], start=False, stop=True,
                                      skip_group_check=True)
                        last.then_inc(w1_used[r], 1)
                    pe.wait_ge(mid_ready, CHUNKS0 * g + r + 1)
                    for k in range(KT):
                        last = t_.transpose(tiles(5)[:, k], mid[:, P * k:P * k + P], ident[:])
                    last.then_inc(midT_ps, 1)
                    pe.wait_ge(midT_ready, CHUNKS0 * g + r + 1)
                    for k in range(KT):
                        pe.wait_ge(ld_u2[r][k], 16 * (g + 1))
                        for j in range(EG):
                            own = slice(TOP0 * j, TOP0 * j + TOP0)
                            last = mm(bank(2)[own], midT[:, k, own], unit_w2[r][:, k, j], start=False, stop=True,
                                      skip_group_check=True)
                        last.then_inc(w2_used[r], 1)
                pe.wait_ge(unit_ready, g + 1)
                pe.wait_ge(scatter_ready, g + 1)
                mm(bank(7), scatter[:], unit_out[:], start=False, stop=True, skip_group_check=True).then_inc(ffn0_ps, 1)

            transpose_x(2, 0)
            pe.wait_ge(poly_ready, 4)
            neighbours(xn, polyT)
            pe.wait_ge(xnT_ready, 3)
            for i, done, w in ((1, k_ps, wk_sb), (2, v_ps, wv_sb)):
                pe.wait_ge(ld_qkv[i], 16)
                project_kv(2 + i, done, w)
            pe.wait_ge(ld_qkv[0], 16)
            project_q(wq_sb)
            keys_values(1)
            pe.wait_ge(ld_l1_rows, 32)
            pe.wait_ge(polyrow_ready, 1)
            mm(bank(7), poly_rows[:], gnn_b_row[:], start=True, stop=False)
            pe.wait_ge(ah_ready, 3)
            mm(bank(1), ones[0:1, :], bout_row[:], start=True, stop=False)
            pe.wait_ge(ld_gnn_w, 16)
            mm(bank(7), ahT[:, 0], gnn_w_sb[:, 0], start=False, stop=False)
            attend(1)
            for k in range(1, KT):
                last = mm(bank(7), ahT[:, k], gnn_w_sb[:, k], start=False, stop=(k == KT - 1))
            last.then_inc(gnn1_ps, 1)
            pe.wait_ge(mix_ready, 2)
            for k in range(KT):
                last = t_.transpose(tiles(0)[:, k], mix[:, P * k:P * k + P], ident[:])
            last.then_inc(mixT_ps, 1)
            pe.wait_ge(ld_wout, 16)
            pe.wait_ge(mixT_ready, 1)
            for k in range(KT):
                last = mm(bank(1), mixT[:, k], wout_sb[:, k], start=False, stop=(k == KT - 1))
            last.then_inc(wout_ps, 1)

            transpose_x(3, 4)

            def up(s, stage, i, lo_done, free, done):
                n = even(s.cols[1])
                if s.last:
                    raw, landed = (w1_raw, ld_w1) if stage is s1 else (w2_raw, ld_w2)
                    c0, n = s.cols
                    pe.wait_ge(landed[s.j], 16 * (s.expert + 1))
                    pe.wait_ge(free, s.g - 1)
                    for k in range(KT):
                        last = mm(bank(i + s.par)[:, 0:n], xnT[:, k], raw[:, k, c0:c0 + n], start=(k == 0), stop=(k == KT - 1))
                    last.then_inc(done, 1)
                    return
                pe.wait_ge(lo_done, s.g + 1)
                if s.n > 1:
                    pe.wait_ge(free, s.g - 1)
                hi, lo = stage[s.par]
                for k in range(KT):
                    for xT, w in ((xT_hi, hi), (xT_hi, lo), (xT_lo, hi)):
                        last = mm(bank(i + s.par)[:, 0:n], xT[:, k], w[:, k, 0:n], start=(k == 0 and w is hi and xT is xT_hi),
                                  stop=(k == KT - 1 and xT is xT_lo))
                last.then_inc(done, 1)

            def transpose_h(s):
                pe.wait_ge(h_ready, s.g + 1)
                if s.n > 1:
                    before = s.before
                    if before.whole:
                        pe.wait_ge(hT_hi_ready, before.g + 1)
                    else:
                        pe.wait_ge(hT_lo_ready, before.g3 + 1)
                for k in range(s.tiles):
                    rows = min(P, s.cols[1] - P * k)
                    last = t_.transpose(tiles(4 + s.par)[0:rows, k], h[s.par][:, P * k:P * k + rows], ident[:])
                last.then_inc(hT_ps, 1)

            def down(s):
                if s.whole:
                    pe.wait_ge(hT_hi_ready, s.g + 1)
                    pe.wait_ge(ld_w3[s.j], 48 * (s.expert + 1))
                    for k in range(s.tiles):
                        rows = min(P, s.cols[1] - P * k)
                        last = mm(bank(6), hT_32[0:rows, k], w3_raw[0:rows, s.t0 + k], start=False,
                                  stop=(s.last and k == s.tiles - 1))
                else:
                    pe.wait_ge(hT_lo_ready, s.g3 + 1)
                    pe.wait_ge(s3_lo, s.g3 + 1)
                    (h_hi, h_lo), (w_hi, w_lo) = hT[s.par], s3[s.par]
                    for k in range(KT):
                        for a, w in ((h_hi, w_hi), (h_hi, w_lo), (h_lo, w_hi)):
                            last = mm(bank(6), a[:, k], w[:, k], start=(s.first and k == 0 and a is h_hi and w is w_hi),
                                      stop=False)
                last.then_inc(down_done, 1)

            def chunk(n, i=None):
                s = Step(n, i)
                up(s, s1, 0, s1_lo, act_ready, a_done)
                if n > 0:
                    transpose_h(Step(n - 1, i))
                up(s, s2, 2, s2_lo, h_ready, b_done)
                if n > 0:
                    down(Step(n - 1, i))

            pe.wait_ge(x_lo_ready, 1)
            for n in range(NC):
                chunk(n)
                if n == 0:
                    pe.wait_ge(xnT_ready, 4)
                    for k in range(KT):
                        mm(bank(7)[:, 0:E1], xnT[:, k], gate1_w[:, k], start=(k == 0), stop=False)
                    mm(bank(7)[:, 0:E1], ones[0:1, :], gate1_b[:], start=False, stop=True).then_inc(gate1_ps, 1)
            with pe.Fori(0, E1 // 2 - 1) as i:
                for n in range(NC, 3 * NC):
                    chunk(n, i)
            for n in range(NC, 3 * NC):
                chunk(n, E1 // 2 - 1)
            transpose_h(Step(G_ALL - 1))
            down(Step(G_ALL - 1))


class Step:

    def __init__(self, n, i=None):
        self.n = n
        self.g = n if i is None else 2 * NC * i + n
        self.expert = n // NC if i is None else 2 * i + n // NC
        self.j = n % NC
        self.par = n % 2
        self.cols = CHUNK[self.j]
        self.full, self.rest = self.cols[1] // P, self.cols[1] % P
        self.tiles = self.full + (self.rest > 0)
        self.t0 = self.cols[0] // P
        self.whole = self.j >= SPLIT3
        self.g3 = SPLIT3 * self.expert + self.j
        self.before = Step(n - 2, i) if n > 1 else None
        self.first = i is None and n == 0
        self.last = isinstance(self.g, int) and self.g == G_ALL - 1


_INS = ["x", "src", "dst", "edge_weight", "L0_gnn_W_gcn", "L0_gnn_b_gcn", "L0_gnn_W_mlp", "L0_gnn_b_mlp",
        "L0_mix_Wq", "L0_mix_Wkv", "L0_ffn_Wg", "L0_ffn_W1", "L0_ffn_b1", "L0_ffn_W2", "L0_ffn_b2", "L1_gnn_W",
        "L1_gnn_b", "L1_gnn_diffusion_weights", "L1_mix_W_qkv", "L1_mix_W_out", "L1_mix_b_out", "L1_ffn_gate_w",
        "L1_ffn_routing_bias", "L1_ffn_w1", "L1_ffn_w2", "L1_ffn_w3", "L1_ffn_sw1", "L1_ffn_sw2", "L1_ffn_sw3"]


def kernel(**inputs):
    import concourse.bacc as bacc
    from concourse.bass_utils import run_bass_kernel_spmd

    nc = bacc.Bacc("TRN2", target_bir_lowering=False, num_devices=1)
    arrays, args = {}, []
    for name in _INS:
        a = np.ascontiguousarray(inputs[name])
        arrays[f"in_{name}"] = a
        args.append(nc.dram_tensor(f"in_{name}", a.shape, mybir.dt.from_np(a.dtype), kind="ExternalInput").ap())
    args.append(nc.dram_tensor("out_x", (P, D), F32, kind="ExternalOutput").ap())
    gps_kernel(nc, *args)
    r = run_bass_kernel_spmd(nc, [arrays], core_ids=[0])
    return r.results[0]["out_x"]
```
